# Optimizing a Trainium2 kernel written in Bass

```python
import numpy as np
import jax
import jax.numpy as jnp

def _softmax(x, axis=-1):
    return jax.nn.softmax(x, axis=axis)

def _gelu(x):
    return jax.nn.gelu(x, approximate=True)

def _silu(x):
    return jax.nn.silu(x)

def _sigmoid(x):
    return jax.nn.sigmoid(x)

def _layernorm(x, axis=-1, eps=1e-05):
    m = jnp.mean(x, axis=axis, keepdims=True)
    v = jnp.var(x, axis=axis, keepdims=True)
    return (x - m) / jnp.sqrt(v + eps)

def _scatter_add(tgt, idx, src, axis=0):
    return tgt.at[idx].add(src)

def _segment_sum(src, seg, n):
    return jax.ops.segment_sum(src, seg, n)
kernel_name = 'mk_xattn_ffn_d1_seqx_r8_75fbd6'

def setup_inputs(seed: int=0):
    np.random.seed(seed)
    _w = jnp.asarray

    def _rec_inputs():
        import jax
        import jax.numpy as jnp
        _rk = jax.random.key(seed)
        x = 0.002226 + 0.9996 * jax.random.normal(jax.random.fold_in(_rk, 1), (2, 512, 128), jnp.float32)
        _lenS = 512 - jax.random.randint(jax.random.fold_in(_rk, 7), (2,), 0, max(1, 512 // 4) + 1, jnp.int32)
        _lenS2 = 154 - jax.random.randint(jax.random.fold_in(_rk, 8), (2,), 0, max(1, 154 // 4) + 1, jnp.int32)
        _ctx_1024P = jax.random.normal(jax.random.fold_in(_rk, 11), (2, 16, 128), jnp.float32)
        _ctx_1024c = jax.random.dirichlet(jax.random.fold_in(_rk, 511), 0.3 * jnp.ones((16,), jnp.float32), (2, 154))
        _ctx_1024t = jnp.einsum('bsk,bkd->bsd', _ctx_1024c, _ctx_1024P)
        _ctx_1024t = _ctx_1024t * jax.lax.rsqrt(jnp.mean(jnp.square(_ctx_1024t)) + 1e-12) * 0.953939
        ctx_1024 = -0.000125008 + 0.999885 * (_ctx_1024t + 0.3 * jax.random.normal(jax.random.fold_in(_rk, 611), (2, 154, 128), jnp.float32))
        return (x, ctx_1024)
    x, ctx_1024 = _rec_inputs()

    def _L0_xattn_setup():
        import jax, jax.numpy as jnp
        import numpy as np
        EPS = 1e-05

        def layer_norm(x, g, b):
            mu = jnp.mean(x, axis=-1, keepdims=True)
            var = jnp.var(x, axis=-1, keepdims=True)
            return (x - mu) * jax.lax.rsqrt(var + EPS) * g + b
        key = jax.random.key(seed)
        ks = jax.random.split(key, 8)
        dim, heads, dim_head = (128, 16, 64)
        inner = heads * dim_head
        b, n, m = (8, 512, 64)
        s = dim ** (-0.5)
        return {'x': jax.random.normal(ks[0], (b, n, dim), jnp.float32), 'latents': jax.random.normal(ks[1], (b, m, dim), jnp.float32), 'ln_m_g': jnp.ones((dim,), jnp.float32), 'ln_m_b': jnp.zeros((dim,), jnp.float32), 'ln_l_g': jnp.ones((dim,), jnp.float32), 'ln_l_b': jnp.zeros((dim,), jnp.float32), 'Wq': jax.random.normal(ks[2], (dim, inner), jnp.float32) * s, 'Wkv': jax.random.normal(ks[3], (dim, 2 * inner), jnp.float32) * s, 'Wout': jax.random.normal(ks[4], (inner, dim), jnp.float32) * s}
    _L0_xattn_all = _L0_xattn_setup()
    _L0_xattn_in = {k: v for k, v in _L0_xattn_all.items() if k in ('ln_m_g', 'ln_m_b', 'ln_l_g', 'ln_l_b', 'Wq', 'Wkv', 'Wout')}
    del _L0_xattn_all

    def _L0_ffn_setup():
        import jax, jax.numpy as jnp
        import numpy as np
        E = 8
        D = 128
        H = 256
        TOP_K = 2
        key = jax.random.key(seed)
        k_x, k_g, k_w1, k_w2 = jax.random.split(key, 4)
        B, S = (4, 256)
        inp = {'input': jax.random.normal(k_x, (B, S, D), dtype=jnp.float32), 'Wg': jax.random.normal(k_g, (D, E), dtype=jnp.float32) * 0.02, 'W1': jax.random.normal(k_w1, (E, D, H), dtype=jnp.float32) * 0.02, 'b1': jnp.zeros((E, H), dtype=jnp.float32), 'W2': jax.random.normal(k_w2, (E, H, D), dtype=jnp.float32) * 0.02, 'b2': jnp.zeros((E, D), dtype=jnp.float32)}
        return inp
    _L0_ffn_all = _L0_ffn_setup()
    _L0_ffn_in = {k: v for k, v in _L0_ffn_all.items() if k in ('Wg', 'W1', 'b1', 'W2', 'b2')}
    del _L0_ffn_all
    return {'x': x, 'ctx_1024': ctx_1024, 'L0_xattn_ln_m_g': _L0_xattn_in['ln_m_g'], 'L0_xattn_ln_m_b': _L0_xattn_in['ln_m_b'], 'L0_xattn_ln_l_g': _L0_xattn_in['ln_l_g'], 'L0_xattn_ln_l_b': _L0_xattn_in['ln_l_b'], 'L0_xattn_Wq': _L0_xattn_in['Wq'], 'L0_xattn_Wkv': _L0_xattn_in['Wkv'], 'L0_xattn_Wout': _L0_xattn_in['Wout'], 'L0_ffn_Wg': _L0_ffn_in['Wg'], 'L0_ffn_W1': _L0_ffn_in['W1'], 'L0_ffn_b1': _L0_ffn_in['b1'], 'L0_ffn_W2': _L0_ffn_in['W2'], 'L0_ffn_b2': _L0_ffn_in['b2']}

def reference(x, ctx_1024, L0_xattn_ln_m_g, L0_xattn_ln_m_b, L0_xattn_ln_l_g, L0_xattn_ln_l_b, L0_xattn_Wq, L0_xattn_Wkv, L0_xattn_Wout, L0_ffn_Wg, L0_ffn_W1, L0_ffn_b1, L0_ffn_W2, L0_ffn_b2):
    import jax
    import jax.numpy as jnp

    def _L0_xattn_ref(x, latents, ln_m_g, ln_m_b, ln_l_g, ln_l_b, Wq, Wkv, Wout):
        import jax, jax.numpy as jnp
        import numpy as np
        EPS = 1e-05

        def layer_norm(x, g, b):
            mu = jnp.mean(x, axis=-1, keepdims=True)
            var = jnp.var(x, axis=-1, keepdims=True)
            return (x - mu) * jax.lax.rsqrt(var + EPS) * g + b
        heads, dim_head = (16, 64)
        scale = dim_head ** (-0.5)
        x = layer_norm(x, ln_m_g, ln_m_b)
        lat = layer_norm(latents, ln_l_g, ln_l_b)
        b, m, _ = lat.shape
        q = lat @ Wq
        kv_input = jnp.concatenate([x, lat], axis=1)
        kv = kv_input @ Wkv
        k, v = jnp.split(kv, 2, axis=-1)

        def split_heads(t):
            return t.reshape(t.shape[0], t.shape[1], heads, dim_head).transpose(0, 2, 1, 3)
        q, k, v = (split_heads(q), split_heads(k), split_heads(v))
        dots = jnp.einsum('bhid,bhjd->bhij', q, k) * scale
        attn = jax.nn.softmax(dots, axis=-1)
        out = jnp.einsum('bhij,bhjd->bhid', attn, v)
        out = out.transpose(0, 2, 1, 3).reshape(b, m, heads * dim_head)
        return out @ Wout

    def _L0_ffn_ref(input, Wg, W1, b1, W2, b2):
        import jax, jax.numpy as jnp
        import numpy as np
        E = 8
        D = 128
        H = 256
        TOP_K = 2
        logits = jnp.einsum('bsd,de->bse', input, Wg)
        probs = jax.nn.softmax(logits, axis=-1)
        top_vals, top_idx = jax.lax.top_k(probs, TOP_K)
        top_vals = top_vals / jnp.sum(top_vals, axis=-1, keepdims=True)
        onehot = jax.nn.one_hot(top_idx, E, dtype=input.dtype)
        mask = jnp.sum(onehot, axis=2)
        scores = jnp.sum(onehot * top_vals[..., None], axis=2)
        xm = input[None] * jnp.moveaxis(mask, -1, 0)[..., None]
        h = jnp.einsum('ebsd,edh->ebsh', xm, W1) + b1[:, None, None, :]
        h = jax.nn.relu(h)
        y = jnp.einsum('ebsh,ehd->ebsd', h, W2) + b2[:, None, None, :]
        out = jnp.sum(y * jnp.moveaxis(scores, -1, 0)[..., None], axis=0)
        return out
    x = x + _L0_xattn_ref(ctx_1024, _layernorm(x, axis=-1), L0_xattn_ln_m_g, L0_xattn_ln_m_b, L0_xattn_ln_l_g, L0_xattn_ln_l_b, L0_xattn_Wq, L0_xattn_Wkv, L0_xattn_Wout)
    x = x + _L0_ffn_ref(_layernorm(x, axis=-1), L0_ffn_Wg, L0_ffn_W1, L0_ffn_b1, L0_ffn_W2, L0_ffn_b2)
    return x

_drawn_inputs = setup_inputs


def setup_inputs(seed=0):
    import zlib

    import numpy as np

    out = dict(_drawn_inputs(seed))
    spreads = {'L0_xattn_ln_m_g': (1.0, 0.2),
     'L0_xattn_ln_m_b': (0.0, 0.1),
     'L0_xattn_ln_l_g': (1.0, 0.2),
     'L0_xattn_ln_l_b': (0.0, 0.1),
     'L0_ffn_b1': (0.0, 0.619),
     'L0_ffn_b2': (0.0, 0.1)}
    factors = {}
    for name, (base, spread) in spreads.items():
        noise = np.random.default_rng([zlib.crc32(name.encode()), seed]).standard_normal(out[name].shape)
        drawn = base * np.exp(spread * noise) if base else spread * noise
        out[name] = jnp.asarray(drawn.astype(out[name].dtype))
    for name, factor in factors.items():
        out[name] = (out[name] * factor).astype(out[name].dtype)
    return out
```

```python
from contextlib import ExitStack

import concourse.bass as bass
from concourse import mybir

F32 = mybir.dt.float32
F32R = mybir.dt.float32r
ALU = mybir.AluOpType
ACT = mybir.ActivationFunctionType
AX = mybir.AxisListType

P = 128
B, N, D = 2, 512, 128
M = 154
H, HD = 16, 64
PAIRS = H // 2
STEPS = PAIRS * B
J = N + M
JP = J + 2
JH = J // 2
QT = N // P
KT = 6
KP = J // KT
TILES = 2 * QT
CT = 2
CP = M // CT
E, HID, TOPK = 8, 256, 2
HC = HID // P
EPS = 1e-5
SCALE = HD ** -0.5

TASKS = ["S0", "S1", "Q", "S2", "S3", "K0", "S4", "S5", "K1", "S6", "S7", "V"]
TURNS = {3: [0, 1], 4: [2], 5: [3], 6: [4, 5], 7: [6], 8: [7], 9: [8, 9], 10: [10], 11: [11]}
PVS = {5: [0], 7: [1], 8: [2], 10: [3], 11: [4]}
PV_LATE = 1
O_COPY = 2
RECIPS = {3: 0, 6: 1, 9: 2}
RECIP_LATE = 0
SPLIT_V = 1
SPLIT_QK = 9
RING = 4


def has_task(last, j):
    return not (last and TASKS[j][0] in "QK")


def xattn_moe(nc, x, ctx_in, g_m, b_m, g_l, b_l, wq, wkv, wout, wg, w1, b1, w2, b2, out):
    with ExitStack() as stack:
        def sb(name, shape, dt=F32):
            return stack.enter_context(nc.sbuf_tensor(name, shape, dt))

        def ps(name, shape):
            return stack.enter_context(nc.psum_tensor(name, shape, F32))

        def sem(name):
            return stack.enter_context(nc.semaphore(name))

        x_tok = sb("x_tok", [P, B, QT, D])
        ctx_tok = sb("ctx_tok", [CP, B, CT, D])
        rows = sb("rows", [E * HC + 4, P])
        cols = sb("cols", [P, E * HC + 4])
        ident = sb("ident", [P, P])
        earlier = sb("earlier", [P, E, E])
        half_power = sb("half_power", [P, QT + CT])
        stats = sb("stats", [P, B, QT + CT, 6])
        moments = sb("moments", [P, B, QT + CT, 2])
        var_eps = sb("var_eps", [P, B, QT + CT])
        rstd = sb("rstd", [P, B, QT + CT])
        normed = sb("normed", [P, B, QT + CT, D])
        kv_t = sb("kv_t", [P, B, JP])
        kv_hi = sb("kv_hi", [P, B, JP], F32R)
        kv_lo = sb("kv_lo", [P, B, JP], F32R)
        wqk_raw = sb("wqk_raw", [P, 2, P])
        wqk_hi = sb("wqk_hi", [P, 2 * 2, 2, HD], F32R)
        wqk_lo = sb("wqk_lo", [P, 2 * 2, 2, HD], F32R)
        wv_raw = sb("wv_raw", [P, P])
        wv_hi = sb("wv_hi", [P, P], F32R)
        wv_lo = sb("wv_lo", [P, P], F32R)
        q_hi = sb("q_hi", [P, B, 2, N], F32R)
        q_lo = sb("q_lo", [P, B, 2, N], F32R)
        k_st = sb("k_st", [P, B, 2, JP], F32R)
        v_sb = sb("v_sb", [P, B, KT, P])
        neg_max = sb("neg_max", [P, B, TILES])
        sums = sb("sums", [P, B, TILES])
        recips = sb("recips", [P, B, TILES])
        probs = sb("probs", [P, B, TILES, J])
        ring = sb("ring", [P, RING, N])
        o_t = sb("o_t", [P, B, PAIRS, N])
        wout_sb = sb("wout_sb", [P, PAIRS, D])
        w1_sb = sb("w1_sb", [P, E, HID])
        w1_hi = sb("w1_hi", [P, E, HID], F32R)
        w1_lo = sb("w1_lo", [P, E, HID], F32R)
        w2_sb = sb("w2_sb", [P, E * HC, D])
        wg_sb = sb("wg_sb", [P, E])
        b2_sb = sb("b2_sb", [E, D])
        acc = sb("acc", [P, B, QT, D])
        g_neg = sb("g_neg", [P, B, QT])
        g_sub = sb("g_sub", [P, B, QT, E])
        g_exp = sb("g_exp", [P, B, QT, E])
        g_sum = sb("g_sum", [P, B, QT])
        g_rec = sb("g_rec", [P, B, QT])
        g_prob = sb("g_prob", [P, B, QT, E])
        g_gt = sb("g_gt", [P, B, QT, E, E])
        g_eq = sb("g_eq", [P, B, QT, E, E])
        g_rank = sb("g_rank", [P, B, QT, E])
        g_top = sb("g_top", [P, B, QT, E])
        g_tsum = sb("g_tsum", [P, B, QT])
        g_trec = sb("g_trec", [P, B, QT])
        score = sb("score", [P, B, QT, E])
        score_t = sb("score_t", [E, B, N])

        slots = ps("slots", [P, 2, 2, N])
        turned = ps("turned", [P, 3, N])
        o_ps = ps("o_ps", [P, N])
        hid_ps = slots[:, :, :, :].rearrange("p a b n -> p (a b) n")

        x_in = [sem(f"x_in{b}") for b in range(B)]
        ctx_loaded = sem("ctx_loaded")
        rows_loaded = sem("rows_loaded")
        wqk_loaded = sem("wqk_loaded")
        wv_loaded = sem("wv_loaded")
        w1_loaded = sem("w1_loaded")
        tail_loaded = sem("tail_loaded")
        consts = sem("consts")
        cols_turned = sem("cols_turned")
        cols_ready = sem("cols_ready")
        setup_p = sem("setup_p")
        setup_v = sem("setup_v")
        var_ready = sem("var_ready")
        rstd_ready = sem("rstd_ready")
        normed_ready = sem("normed_ready")
        norm_turned = sem("norm_turned")
        kv_ready = sem("kv_ready")
        kv_hi_ready = sem("kv_hi_ready")
        kv_lo_ready = sem("kv_lo_ready")
        pads = sem("pads")
        wqk_hi_ready = sem("wqk_hi_ready")
        wqk_split = sem("wqk_split")
        wv_hi_ready = sem("wv_hi_ready")
        wv_split = sem("wv_split")
        scores_ready = sem("scores_ready")
        qk_ready = sem("qk_ready")
        v_ready = sem("v_ready")
        max_done = sem("max_done")
        exp_done = sem("exp_done")
        recip_done = sem("recip_done")
        prob_done = sem("prob_done")
        qk_hi_done = sem("qk_hi_done")
        qk_lo_done = sem("qk_lo_done")
        v_copied = sem("v_copied")
        turn_ready = sem("turn_ready")
        even_copied = sem("even_copied")
        odd_copied = sem("odd_copied")
        pv_done = sem("pv_done")
        o_copied = sem("o_copied")
        out_proj = sem("out_proj")
        x1_ready = sem("x1_ready")
        w1_split = sem("w1_split")
        w1_hi_ready = sem("w1_hi_ready")
        x2_turned = sem("x2_turned")
        x2_copied = sem("x2_copied")
        x2_hi = sem("x2_hi")
        x2_lo = sem("x2_lo")
        logits_ready = sem("logits_ready")
        gate_sub = sem("gate_sub")
        gate_exp = sem("gate_exp")
        gate_v = sem("gate_v")
        score_ready = sem("score_ready")
        score_turned = sem("score_turned")
        score_copied = sem("score_copied")
        bias_ready = sem("bias_ready")
        acc_ready = sem("acc_ready")
        hid_ready = sem("hid_ready")
        relu_done = sem("relu_done")
        y_ready = sem("y_ready")
        acc_v = sem("acc_v")
        stored = sem("stored")

        block = stack.enter_context(nc.Block())

        wq_pair = wq.rearrange("d (r c) -> d r c", c=P)
        wkv_pair = wkv.rearrange("d (r c) -> d r c", c=P)

        raw_twice = wqk_raw[:, :, :].rearrange("p w (h c) -> p (w h) c", h=2).unsqueeze(2) \
            .to_broadcast([P, 2 * 2, 2, HD])

        def in_step(run):
            def for_engine(eng):
                for b in range(B):
                    run(0, b, b, b, False)
                with eng.Fori(1, PAIRS - 1) as pair:
                    for b in range(B):
                        run(pair, b, 2 * pair + b, B, False)
                for b in range(B):
                    run(PAIRS - 1, b, 2 * (PAIRS - 1) + b, B, b == B - 1)
            return for_engine

        @block.sync
        def _(sp):
            for b in range(B):
                sp.dma_start(x_tok[:, b], x[b].rearrange("(t p) d -> p t d", p=P)).then_inc(x_in[b], 16)
                if b == 0:
                    sp.dma_start(ctx_tok[:, :, :, :].rearrange("p b t d -> p (b t) d"),
                                 ctx_in.rearrange("b (t p) d -> p (b t) d", p=CP)).then_inc(ctx_loaded, 16)
            sp.dma_start(wv_raw[:, :], wkv_pair[:, PAIRS]).then_inc(wv_loaded, 16)
            with sp.Fori(1, PAIRS) as pair:
                sp.wait_ge(wqk_split, pair)
                sp.dma_start(wqk_raw[:, 0], wq_pair[:, bass.ds(pair, 1)]).then_inc(wqk_loaded, 16)
                sp.dma_start(wqk_raw[:, 1], wkv_pair[:, bass.ds(pair, 1)]).then_inc(wqk_loaded, 16)
                sp.wait_ge(wv_split, pair)
                sp.dma_start(wv_raw[:, :], wkv_pair[:, bass.ds(pair + PAIRS, 1)]).then_inc(wv_loaded, 16)
            for b in range(B):
                sp.wait_ge(acc_v, QT * E * (b + 1))
                sp.dma_start(out[b].rearrange("(t p) d -> p t d", p=P), acc[:, b]).then_inc(stored, 16)
            sp.wait_ge(stored, 16 * B)

        @block.tensor
        def _(pe):
            def three(out_ap, st_hi, st_lo, mv_hi, mv_lo):
                pe.matmul(out_ap, st_hi, mv_hi, start=True, stop=False)
                pe.matmul(out_ap, st_hi, mv_lo, start=False, stop=False)
                return pe.matmul(out_ap, st_lo, mv_hi, start=False, stop=True)

            def slot_free(step, j, first, last):
                back = j - 2
                while back >= 0 and not has_task(last, back):
                    back -= 2
                prev = 0
                if back < 0:
                    if first == 0:
                        pe.wait_ge(qk_lo_done, 3 if j % 2 == 0 else 2)
                        return
                    back, prev = back + 12, 1
                kind = TASKS[back]
                if kind[0] == "S":
                    pe.wait_ge(exp_done, TILES * (step - prev) + int(kind[1]) + 1)
                elif kind == "V":
                    pe.wait_ge(v_copied, step - prev + 1)
                else:
                    pe.wait_ge(qk_lo_done, 3 * (step - prev + 1) + ["Q", "K0", "K1"].index(kind) + 1)

            def scores(b, step, n, slot):
                h, t = n // QT, n % QT
                if t == 0:
                    pe.wait_ge(qk_lo_done, 3 * step + 2 + h)
                for half in range(2):
                    o = slots[:, slot, half, 0:JH + 1]
                    k = k_st[:, b, h, half * JH:half * JH + JH + 1]
                    pe.matmul(o, q_hi[:, b, h, t * P:(t + 1) * P], k, start=True, stop=False)
                for half in range(2):
                    o = slots[:, slot, half, 0:JH + 1]
                    k = k_st[:, b, h, half * JH:half * JH + JH + 1]
                    mm = pe.matmul(o, q_lo[:, b, h, t * P:(t + 1) * P], k, start=False, stop=True)
                mm.then_inc(scores_ready, 1)

            def doubled(w, which, h):
                return w[:, 2 * which + h].rearrange("p a c -> p (a c)")

            def project_q(b, slot):
                for h in range(2):
                    mm = three(slots[:, slot, h, :], doubled(wqk_hi, 0, h), doubled(wqk_lo, 0, h),
                               kv_hi[:, b, 0:N], kv_lo[:, b, 0:N])
                mm.then_inc(qk_ready, 1)

            def project_k(b, h, slot):
                for half in range(2):
                    at = slice(half * JH, half * JH + JH + 1)
                    mm = three(slots[:, slot, half, 0:JH + 1], doubled(wqk_hi, 1, h), doubled(wqk_lo, 1, h),
                               kv_hi[:, b, at], kv_lo[:, b, at])
                mm.then_inc(qk_ready, 1)

            def project_v(b, slot):
                flat = slots[:, slot].rearrange("p a n -> p (a n)")
                for kt in range(KT):
                    at = slice(kt * KP, (kt + 1) * KP)
                    mm = three(flat[0:KP, kt * P:(kt + 1) * P], kv_hi[:, b, at], kv_lo[:, b, at],
                               wv_hi[:, :], wv_lo[:, :])
                mm.then_inc(v_ready, 1)

            def turn(b, of, i, no_earlier=False):
                kt, h = i // 2, i % 2
                if i < 2:
                    pe.wait_ge(prob_done, TILES * of + QT * (h + 1))
                g = i - 3
                if g >= 0 or not no_earlier:
                    pe.wait_ge(even_copied if g % 2 == 0 else odd_copied, 6 * of + g // 2 + 1)
                for t in range(QT):
                    mm = pe.transpose(turned[0:KP, i % 3, t * P:(t + 1) * P],
                                      probs[:, b, h * QT + t, kt * KP:(kt + 1) * KP], ident[:, :])
                mm.then_inc(turn_ready, 1)

            def pv(b, of, kt, no_earlier=False):
                if kt == 0:
                    pe.wait_ge(v_copied, of + 1)
                    if not no_earlier:
                        pe.wait_ge(o_copied, of)
                pe.wait_ge(even_copied, 6 * of + kt + 1)
                pe.wait_ge(odd_copied, 6 * of + kt + 1)
                for h in range(2):
                    mm = pe.matmul(o_ps[h * HD:(h + 1) * HD, :], v_sb[0:KP, b, kt, h * HD:(h + 1) * HD],
                                   ring[0:KP, (2 * kt + h) % RING, :], start=(kt == 0), stop=(kt == KT - 1))
                mm.then_inc(pv_done, 1)

            pe.wait_ge(consts, 1)
            pe.wait_ge(rows_loaded, 16 * 5)
            pe.transpose(turned[:, 2, 0:E * HC + 4], rows[:, :], ident[0:E * HC + 4, 0:E * HC + 4]) \
              .then_inc(cols_turned, 1)
            for b in range(B):
                pe.wait_ge(normed_ready, (QT + CT) * (b + 1))
                if b == 1:
                    pe.wait_ge(kv_ready, 2)
                for t in range(QT):
                    pe.transpose(turned[:, 0, t * P:(t + 1) * P], normed[:, b, t, :], ident[:, :])
                for t in range(CT):
                    mm = pe.transpose(turned[:, 1, t * CP:(t + 1) * CP], normed[0:CP, b, QT + t, :],
                                      ident[0:CP, 0:CP])
                mm.then_inc(norm_turned, 1)
                if b == 0:
                    pe.wait_ge(kv_lo_ready, 1)
                    pe.wait_ge(wqk_split, 1)
                    project_q(0, 0)
                    project_k(0, 0, 1)
                    pe.wait_ge(qk_lo_done, 1)
                    project_k(0, 1, 0)
            pe.wait_ge(pads, B)

            def run(pair, b, step, first, last):
                for j, kind in enumerate(TASKS):
                    slot = j % 2
                    if has_task(last, j):
                        slot_free(step, j, first, last)
                        if kind[0] == "S":
                            scores(b, step, int(kind[1]), slot)
                        elif kind == "Q":
                            if b == 0 and first == 0:
                                pe.wait_ge(kv_lo_ready, 2)
                            if b == 1:
                                pe.wait_ge(wqk_split, pair + 2)
                            project_q(1 - b, slot)
                        elif kind == "V":
                            if b == 0:
                                pe.wait_ge(wv_split, pair + 1)
                            project_v(b, slot)
                        else:
                            project_k(1 - b, int(kind[1]), slot)
                    if j == PV_LATE and first >= 2:
                        pv(b, step - 2, KT - 1)
                    if first >= 1:
                        for kt in PVS.get(j, []):
                            pv(1 - b, step - 1, kt, no_earlier=(first == 1))
                        for i in TURNS.get(j, []):
                            turn(1 - b, step - 1, i, no_earlier=(first == 1))

            in_step(run)(pe)

            def out_project(b, bank):
                for t in range(QT):
                    for r in range(PAIRS):
                        mm = pe.matmul(bank[:, t * P:(t + 1) * P], o_t[:, b, r, t * P:(t + 1) * P],
                                       wout_sb[:, r, :], start=(r == 0), stop=(r == PAIRS - 1))
                mm.then_inc(out_proj, 1)

            def turn_x2(b):
                pe.wait_ge(normed_ready, B * (QT + CT) + QT * (b + 1))
                pe.wait_ge(x2_lo, b) if b else pe.wait_ge(odd_copied, 6 * STEPS)
                if b:
                    pe.wait_ge(acc_ready, 1)
                for t in range(QT):
                    mm = pe.transpose(turned[:, 2, t * P:(t + 1) * P], normed[:, b, t, :], ident[:, :])
                mm.then_inc(x2_turned, 1)

            def logits(b):
                pe.wait_ge(x2_copied, b + 1)
                pe.wait_ge(o_copied, STEPS) if b == 0 else pe.wait_ge(score_copied, 1)
                for t in range(QT):
                    mm = pe.matmul(o_ps[:, t * E:(t + 1) * E], kv_t[:, b, t * P:(t + 1) * P], wg_sb[:, :],
                                   start=True, stop=True)
                mm.then_inc(logits_ready, 1)

            def bias_term(b):
                pe.wait_ge(score_ready, b + 1)
                for t in range(QT):
                    mm = pe.transpose(o_ps[0:E, t * P:(t + 1) * P], score[:, b, t, :], ident[:, :])
                mm.then_inc(score_turned, 1)
                pe.wait_ge(score_copied, b + 1)
                pe.wait_ge(x2_lo, b + 1)
                for t in range(QT):
                    mm = pe.matmul(turned[:, 2, t * P:(t + 1) * P], score_t[:, b, t * P:(t + 1) * P],
                                   b2_sb[:, :], start=True, stop=True)
                mm.then_inc(bias_ready, 1)

            def hidden(g):
                b, e = g // E, g % E
                if g == 0:
                    pe.wait_ge(v_copied, STEPS)
                    pe.wait_ge(x1_ready, B)
                if e == 0:
                    pe.wait_ge(x2_lo, b + 1)
                pe.wait_ge(w1_split, min(g + 1, E))
                for c in range(HC):
                    n = g * HC + c
                    if n >= 4:
                        pe.wait_ge(relu_done, n - 3)
                    three(hid_ps[:, n % 4, :], w1_hi[:, e, c * P:(c + 1) * P], w1_lo[:, e, c * P:(c + 1) * P],
                          kv_hi[:, b, 0:N], kv_lo[:, b, 0:N]).then_inc(hid_ready, 1)

            def expert_out(g):
                e = g % E
                if g >= 2:
                    pe.wait_ge(acc_v, QT * (g - 1))
                pe.wait_ge(relu_done, HC * (g + 1))
                for t in range(QT):
                    for c in range(HC):
                        mm = pe.matmul(turned[:, g % 2, t * P:(t + 1) * P],
                                       ring[:, (g * HC + c) % RING, t * P:(t + 1) * P],
                                       w2_sb[:, e * HC + c, :], start=(c == 0), stop=(c == HC - 1))
                mm.then_inc(y_ready, 1)

            pv(0, STEPS - 2, KT - 1)
            pe.wait_ge(tail_loaded, 16 * 4)
            pe.wait_ge(o_copied, STEPS - 1)
            pe.wait_ge(exp_done, TILES * STEPS)
            out_project(0, slots[:, 0, 0, :])
            for i in range(2 * KT):
                turn(1, STEPS - 1, i)
                if i >= 3 and i % 2 == 1:
                    pv(1, STEPS - 1, i // 2 - 1)
            pv(1, STEPS - 1, KT - 1)
            turn_x2(0)
            pe.wait_ge(o_copied, STEPS)
            pe.wait_ge(v_copied, STEPS)
            out_project(1, slots[:, 1, 0, :])
            logits(0)
            for g in range(B * E):
                hidden(g)
                if g % E == 1:
                    bias_term(g // E)
                if g >= 1:
                    expert_out(g - 1)
                if g == E // 2:
                    turn_x2(1)
                if g == E // 2 + 1:
                    logits(1)
            expert_out(B * E - 1)

        @block.scalar
        def _(act):
            act.dma_start(rows[0:E * HC, :], b1.rearrange("e (c p) -> (e c) p", p=P)).then_inc(rows_loaded, 16)
            for n, v in enumerate([g_l, b_l, g_m, b_m]):
                act.dma_start(rows[E * HC + n:E * HC + n + 1, :], v.rearrange("(a d) -> a d", a=1)) \
                   .then_inc(rows_loaded, 16)
            act.dma_start(wqk_raw[:, 0], wq_pair[:, 0]).then_inc(wqk_loaded, 16)
            act.dma_start(wqk_raw[:, 1], wkv_pair[:, 0]).then_inc(wqk_loaded, 16)
            act.dma_start(w1_sb[:, :, :], w1.rearrange("e d h -> d e h")).then_inc(w1_loaded, 16)
            act.dma_start(wout_sb[:, :, :], wout.rearrange("(r p) d -> p r d", p=P)).then_inc(tail_loaded, 16)
            act.dma_start(w2_sb[:, :, :], w2.rearrange("e (c p) d -> p (e c) d", p=P)).then_inc(tail_loaded, 16)
            act.dma_start(wg_sb[:, :], wg).then_inc(tail_loaded, 16)
            act.dma_start(b2_sb[:, :], b2).then_inc(tail_loaded, 16)

            def split_qk(n):
                act.wait_ge(wqk_loaded, 32 * (n + 1))
                act.copy(wqk_hi[:, :, :, :], raw_twice).then_inc(wqk_hi_ready, 1)

            def split_v(n):
                act.wait_ge(wv_loaded, 16 * (n + 1))
                act.copy(wv_hi[:, :], wv_raw[:, :]).then_inc(wv_hi_ready, 1)

            def q_high(b, slot):
                act.activation(q_hi[:, b], slots[:, slot], ACT.Copy, scale=SCALE).then_inc(qk_hi_done, 1)

            def k_high(b, h, slot):
                act.copy(k_st[:, b, h, 0:J].rearrange("p (a n) -> p a n", a=2), slots[:, slot, :, 0:JH]) \
                   .then_inc(qk_hi_done, 1)

            def copy_turned(of, i, no_earlier):
                act.wait_ge(turn_ready, 2 * KT * of + i + 1)
                if not (no_earlier and i < RING):
                    act.wait_ge(pv_done, KT * of + i // 2 - 1)
                act.copy(ring[0:KP, i % RING, :], turned[0:KP, i % 3, :]).then_inc(even_copied, 1)

            act.wait_ge(cols_turned, 1)
            act.copy(cols[:, :], turned[:, 2, 0:E * HC + 4]).then_inc(cols_ready, 1)
            split_qk(0)
            split_v(0)
            act.wait_ge(kv_ready, 3)
            act.copy(kv_hi[:, 0, :], kv_t[:, 0, :]).then_inc(kv_hi_ready, 1)
            act.wait_ge(qk_ready, 1)
            q_high(0, 0)
            act.wait_ge(qk_ready, 2)
            k_high(0, 0, 1)
            act.wait_ge(qk_ready, 3)
            k_high(0, 1, 0)
            act.wait_ge(kv_ready, 5)
            act.copy(kv_hi[:, 1, :], kv_t[:, 1, :]).then_inc(kv_hi_ready, 1)

            def run(pair, b, step, first, last):
                for j, kind in enumerate(TASKS):
                    slot = j % 2
                    if has_task(last, j):
                        if kind[0] == "S":
                            n = int(kind[1])
                            act.wait_ge(max_done, TILES * step + n + 1)
                            act.activation(probs[:, b, n, :].rearrange("p (a n) -> p a n", a=2),
                                           slots[:, slot, :, 0:JH], ACT.Exp, bias=neg_max[:, b, n:n + 1],
                                           accum_out=sums[:, b, n:n + 1]).then_inc(exp_done, 1)
                        elif kind == "V":
                            act.wait_ge(v_ready, step + 1)
                            act.copy(v_sb[0:KP, b].rearrange("p k c -> p (k c)"),
                                     slots[0:KP, slot].rearrange("p a n -> p (a n)")[:, 0:KT * P]) \
                               .then_inc(v_copied, 1)
                        else:
                            at = ["Q", "K0", "K1"].index(kind)
                            act.wait_ge(qk_ready, 3 * (step + 1) + at + 1)
                            if at == 0:
                                q_high(1 - b, slot)
                            else:
                                k_high(1 - b, at - 1, slot)
                    if first >= 1:
                        for i in TURNS.get(j, []):
                            if i % 2 == 0:
                                copy_turned(step - 1, i, first == 1)
                    if b == 0 and j == SPLIT_V and first >= 2:
                        act.wait_ge(v_ready, step)
                        split_v(pair)
                    if b == 0 and j == SPLIT_QK and not (first == B and isinstance(pair, int)):
                        act.wait_ge(qk_ready, 3 * (step + 2))
                        split_qk(pair + 1)

            in_step(run)(act)
            for i in range(0, 2 * KT, 2):
                copy_turned(STEPS - 1, i, False)

            def gate_exp_of(b):
                act.wait_ge(gate_sub, b + 1)
                act.activation(g_exp[:, b], g_sub[:, b], ACT.Exp).then_inc(gate_exp, 1)

            def copy_x2(b):
                act.wait_ge(x2_turned, b + 1)
                act.copy(kv_t[:, b, 0:N], turned[:, 2, :]).then_inc(x2_copied, 1)
                act.copy(kv_hi[:, b, 0:N], turned[:, 2, :]).then_inc(x2_hi, 1)

            def relu(n):
                act.wait_ge(hid_ready, n + 1)
                if n >= RING:
                    act.wait_ge(y_ready, (n - RING) // HC + 1)
                act.activation(ring[:, n % RING, :], hid_ps[:, n % 4, :], ACT.Relu,
                               bias=cols[:, n % (E * HC):n % (E * HC) + 1]).then_inc(relu_done, 1)

            def copy_scores(b):
                act.wait_ge(score_turned, b + 1)
                act.copy(score_t[:, b, :], o_ps[0:E, :]).then_inc(score_copied, 1)

            act.wait_ge(pv_done, KT * STEPS)
            copy_x2(0)
            gate_exp_of(0)
            for g in range(B * E):
                for c in range(HC):
                    relu(g * HC + c)
                if g % E == 1:
                    copy_scores(g // E)
                if g == E // 2:
                    copy_x2(1)
                if g == E // 2 + 1:
                    gate_exp_of(1)

        @block.vector
        def _(dve):
            own = [0]

            def chained(op):
                op.then_inc(setup_v, 1)
                own[0] += 1
                dve.wait_ge(setup_v, own[0])

            def moments_of(b, tiles):
                for n, tile in tiles:
                    ins = dve.bn_stats(stats[0:tile.shape[0], b, n, :], tile)
                chained(ins)
                for n, tile in tiles:
                    ins = dve.bn_aggr(moments[0:tile.shape[0], b, n, :], stats[0:tile.shape[0], b, n, :])
                chained(ins)

            def apply_norm(b, tiles):
                for n, tile in tiles:
                    r = tile.shape[0]
                    dve.tensor_scalar(normed[0:r, b, n, :], tile, moments[0:r, b, n, 0:1],
                                      rstd[0:r, b, n:n + 1], ALU.subtract, ALU.mult).then_inc(normed_ready, 1)

            chained(dve.memset(moments[:, :, :, :], 1.0))
            dve.memset(kv_t[:, :, J:JP], 0.0).then_inc(kv_ready, 1)
            for b in range(B):
                dve.memset(k_st[:, b, :, J:JP].bitcast(F32), 0.0).then_inc(pads, 1)
            for b in range(B):
                if b == 0:
                    pass
                dve.wait_ge(x_in[b], 16)
                dve.wait_ge(ctx_loaded, 16)
                tiles = [(t, x_tok[:, b, t, :]) for t in range(QT)] + \
                        [(QT + t, ctx_tok[:, b, t, :]) for t in range(CT)]
                moments_of(b, tiles)
                dve.tensor_scalar(var_eps[:, b, 0:QT], moments[:, b, 0:QT, 1], 1.0 + EPS, EPS * EPS,
                                  ALU.mult, ALU.add).then_inc(var_ready, 1)
                dve.tensor_scalar(var_eps[:, b, QT:QT + CT], moments[:, b, QT:QT + CT, 1], EPS, None,
                                  ALU.add).then_inc(var_ready, 1)
                if b == 0:
                    dve.wait_ge(wqk_hi_ready, 1)
                    dve.tensor_tensor(wqk_lo[:, :, :, :], raw_twice, wqk_hi[:, :, :, :].bitcast(F32),
                                      ALU.subtract).then_inc(wqk_split, 1)
                    dve.wait_ge(wv_hi_ready, 1)
                    dve.tensor_tensor(wv_lo[:, :], wv_raw[:, :], wv_hi[:, :].bitcast(F32),
                                      ALU.subtract).then_inc(wv_split, 1)
                dve.wait_ge(rstd_ready, b + 1)
                apply_norm(b, tiles)
                dve.wait_ge(norm_turned, b + 1)
                if b == 0:
                    dve.wait_ge(cols_ready, 1)
                g = E * HC
                dve.tensor_scalar(kv_t[:, b, 0:N], turned[:, 0, :], cols[:, g:g + 1], cols[:, g + 1:g + 2],
                                  ALU.mult, ALU.add).then_inc(kv_ready, 1)
                dve.tensor_scalar(kv_t[:, b, N:J], turned[:, 1, 0:M], cols[:, g + 2:g + 3],
                                  cols[:, g + 3:g + 4], ALU.mult, ALU.add).then_inc(kv_ready, 1)
                dve.wait_ge(kv_hi_ready, b + 1)
                dve.tensor_tensor(kv_lo[:, b, :], kv_t[:, b, :], kv_hi[:, b, :].bitcast(F32), ALU.subtract) \
                   .then_inc(kv_lo_ready, 1)
                if b == 0:
                    for at in range(3):
                        dve.wait_ge(qk_hi_done, at + 1)
                        if at == 0:
                            dve.scalar_tensor_tensor(q_lo[:, 0], slots[:, 0], SCALE, q_hi[:, 0].bitcast(F32),
                                                     ALU.mult, ALU.subtract).then_inc(qk_lo_done, 1)
                        else:
                            slot = at % 2
                            low_k = k_st[HD:P, 0, at - 1, 0:J].rearrange("p (a n) -> p a n", a=2)
                            dve.tensor_tensor(low_k, slots[HD:P, slot, :, 0:JH], low_k.bitcast(F32),
                                              ALU.subtract).then_inc(qk_lo_done, 1)

            def copy_turned(of, i, no_earlier):
                dve.wait_ge(turn_ready, 2 * KT * of + i + 1)
                if not (no_earlier and i < RING):
                    dve.wait_ge(pv_done, KT * of + i // 2 - 1)
                dve.tensor_copy(ring[0:KP, i % RING, :], turned[0:KP, i % 3, :]).then_inc(odd_copied, 1)

            def reciprocals(b, step, r):
                dve.wait_ge(exp_done, TILES * step + 2 * r + 2)
                dve.reciprocal(recips[:, b, 2 * r:2 * r + 2], sums[:, b, 2 * r:2 * r + 2]) \
                   .then_inc(recip_done, 1)

            def copy_output(b, of, pair):
                dve.wait_ge(pv_done, KT * (of + 1))
                if isinstance(pair, int):
                    to = o_t[:, b, pair, :]
                else:
                    to = o_t[:, b, bass.ds(pair, 1), :].rearrange("p a n -> p (a n)")
                dve.tensor_copy(to, o_ps[:, :]).then_inc(o_copied, 1)

            def run(pair, b, step, first, last):
                for j, kind in enumerate(TASKS):
                    slot = j % 2
                    if has_task(last, j):
                        if kind[0] == "S":
                            n = int(kind[1])
                            dve.wait_ge(scores_ready, TILES * step + n + 1)
                            dve.tensor_reduce(neg_max[:, b, n:n + 1], slots[:, slot, :, 0:JH], AX.XY, ALU.max,
                                              negate=True).then_inc(max_done, 1)
                        elif kind != "V":
                            at = ["Q", "K0", "K1"].index(kind)
                            dve.wait_ge(qk_hi_done, 3 * (step + 1) + at + 1)
                            if at == 0:
                                dve.scalar_tensor_tensor(q_lo[:, 1 - b], slots[:, slot], SCALE,
                                                         q_hi[:, 1 - b].bitcast(F32), ALU.mult, ALU.subtract) \
                                   .then_inc(qk_lo_done, 1)
                            else:
                                low_k = k_st[HD:P, 1 - b, at - 1, 0:J].rearrange("p (a n) -> p a n", a=2)
                                dve.tensor_tensor(low_k, slots[HD:P, slot, :, 0:JH], low_k.bitcast(F32),
                                                  ALU.subtract).then_inc(qk_lo_done, 1)
                    if j in RECIPS:
                        reciprocals(b, step, RECIPS[j])
                    if j == RECIP_LATE and first >= 1:
                        reciprocals(1 - b, step - 1, 3)
                    if first >= 1:
                        for i in TURNS.get(j, []):
                            if i % 2 == 1:
                                copy_turned(step - 1, i, first == 1)
                    if j == O_COPY and first >= 2:
                        copy_output(b, step - 2, pair - 1)
                    if b == 0 and j == SPLIT_V and first >= 2:
                        dve.wait_ge(wv_hi_ready, pair + 1)
                        dve.tensor_tensor(wv_lo[:, :], wv_raw[:, :], wv_hi[:, :].bitcast(F32),
                                          ALU.subtract).then_inc(wv_split, 1)
                    if b == 0 and j == SPLIT_QK and not (first == B and isinstance(pair, int)):
                        dve.wait_ge(wqk_hi_ready, pair + 2)
                        dve.tensor_tensor(wqk_lo[:, :, :, :], raw_twice, wqk_hi[:, :, :, :].bitcast(F32),
                                          ALU.subtract).then_inc(wqk_split, 1)

            in_step(run)(dve)
            reciprocals(1, STEPS - 1, 3)
            copy_output(0, STEPS - 2, PAIRS - 1)

            def x1_and_moments(b, bank):
                dve.wait_ge(out_proj, b + 1)
                dve.tensor_tensor(acc[:, b].rearrange("p t d -> p (t d)"), bank,
                                  x_tok[:, b].rearrange("p t d -> p (t d)"), ALU.add).then_inc(x1_ready, 1)
                dve.wait_ge(x1_ready, b + 1)
                moments_of(b, [(t, acc[:, b, t, :]) for t in range(QT)])
                dve.tensor_scalar(var_eps[:, b, 0:QT], moments[:, b, 0:QT, 1], EPS, None, ALU.add) \
                   .then_inc(var_ready, 1)

            def norm_x1(b):
                dve.wait_ge(rstd_ready, B + b + 1)
                apply_norm(b, [(t, acc[:, b, t, :]) for t in range(QT)])

            def split_x2(b):
                dve.wait_ge(x2_hi, b + 1)
                dve.tensor_tensor(kv_lo[:, b, 0:N], turned[:, 2, :], kv_hi[:, b, 0:N].bitcast(F32),
                                  ALU.subtract).then_inc(x2_lo, 1)

            def gate_start(b):
                dve.wait_ge(logits_ready, b + 1)
                lg = o_ps[:, 0:QT * E].rearrange("p (t e) -> p t e", e=E)
                chained(dve.tensor_reduce(g_neg[:, b, :], lg, AX.X, ALU.max))
                dve.tensor_tensor(g_sub[:, b], lg, g_neg[:, b, :].unsqueeze(2).to_broadcast([P, QT, E]),
                                  ALU.subtract).then_inc(gate_sub, 1)

            def gate_end(b):
                dve.wait_ge(gate_exp, b + 1)
                chained(dve.tensor_reduce(g_sum[:, b, :], g_exp[:, b], AX.X, ALU.add))
                chained(dve.reciprocal(g_rec[:, b, :], g_sum[:, b, :]))
                chained(dve.tensor_tensor(g_prob[:, b], g_exp[:, b],
                                          g_rec[:, b, :].unsqueeze(2).to_broadcast([P, QT, E]), ALU.mult))
                for t in range(QT):
                    pj = g_prob[:, b, t, :].unsqueeze(1).to_broadcast([P, E, E])
                    pe_ = g_prob[:, b, t, :].unsqueeze(2).to_broadcast([P, E, E])
                    dve.tensor_tensor(g_gt[:, b, t], pj, pe_, ALU.is_gt)
                    ins = dve.tensor_tensor(g_eq[:, b, t], pj, pe_, ALU.is_equal)
                chained(ins)
                first_of = earlier[:, :, :].unsqueeze(1).to_broadcast([P, QT, E, E])
                chained(dve.tensor_tensor(g_eq[:, b], g_eq[:, b], first_of, ALU.mult))
                chained(dve.tensor_tensor(g_gt[:, b], g_gt[:, b], g_eq[:, b], ALU.add))
                chained(dve.tensor_reduce(g_rank[:, b], g_gt[:, b], AX.X, ALU.add))
                chained(dve.scalar_tensor_tensor(g_top[:, b], g_rank[:, b], float(TOPK), g_prob[:, b],
                                                 ALU.is_lt, ALU.mult))
                chained(dve.tensor_reduce(g_tsum[:, b, :], g_top[:, b], AX.X, ALU.add))
                chained(dve.reciprocal(g_trec[:, b, :], g_tsum[:, b, :]))
                dve.tensor_tensor(score[:, b], g_top[:, b],
                                  g_trec[:, b, :].unsqueeze(2).to_broadcast([P, QT, E]), ALU.mult) \
                   .then_inc(score_ready, 1)

            def add_bias(b):
                dve.wait_ge(bias_ready, b + 1)
                dve.tensor_tensor(acc[:, b].rearrange("p t d -> p (t d)"), turned[:, 2, :],
                                  acc[:, b].rearrange("p t d -> p (t d)"), ALU.add).then_inc(acc_ready, 1)
                dve.wait_ge(acc_ready, b + 1)

            def add_expert(g):
                b, e = g // E, g % E
                dve.wait_ge(y_ready, g + 1)
                if e >= 1:
                    dve.wait_ge(acc_v, QT * g)
                for t in range(QT):
                    dve.scalar_tensor_tensor(acc[:, b, t, :], turned[:, g % 2, t * P:(t + 1) * P],
                                             score[:, b, t, e:e + 1], acc[:, b, t, :], ALU.mult, ALU.add) \
                       .then_inc(acc_v, 1)

            x1_and_moments(0, slots[:, 0, 0, :])
            copy_turned(STEPS - 1, 1, False)
            copy_turned(STEPS - 1, 3, False)
            norm_x1(0)
            for i in range(5, 2 * KT, 2):
                copy_turned(STEPS - 1, i, False)
            copy_output(1, STEPS - 1, PAIRS - 1)
            split_x2(0)
            x1_and_moments(1, slots[:, 1, 0, :])
            gate_start(0)
            norm_x1(1)
            gate_end(0)
            for g in range(B * E):
                if g % E == 0:
                    add_bias(g // E)
                add_expert(g)
                if g == E // 2 - 1:
                    split_x2(1)
                if g == E // 2:
                    gate_start(1)
                    gate_end(1)

        @block.gpsimd
        def _(pool):
            ones = pool.memset(ident[:, :], 0.0)
            ones.then_inc(setup_p, 1)
            pool.memset(earlier[:, :, :], 1.0).then_inc(setup_p, 1)
            pool.memset(half_power[:, :], -0.5).then_inc(setup_p, 1)
            pool.wait_ge(setup_p, 3)
            pool.affine_select(out=ident[:, :], in_=ident[:, :], compare_op=ALU.not_equal, fill=1.0,
                               base=0, pattern=[[-1, P]], channel_multiplier=1).then_inc(consts, 1)
            pool.affine_select(out=earlier[:, :, :], in_=earlier[:, :, :], compare_op=ALU.is_ge, fill=0.0,
                               base=-1, pattern=[[1, E], [-1, E]], channel_multiplier=0).then_inc(consts, 1)

            for b in range(B):
                pool.wait_ge(var_ready, 2 * (b + 1))
                pool.tensor_tensor(rstd[:, b, :], var_eps[:, b, :], half_power[:, :], ALU.pow) \
                    .then_inc(rstd_ready, 1)

            def run(pair, b, step, first, last):
                for n in range(TILES):
                    if n % 2 == 0:
                        pool.wait_ge(recip_done, 4 * step + n // 2 + 1)
                    pool.tensor_tensor(probs[:, b, n, :], probs[:, b, n, :],
                                       recips[:, b, n:n + 1].to_broadcast([P, J]), ALU.mult) \
                        .then_inc(prob_done, 1)

            in_step(run)(pool)

            def split_w1(e):
                pool.tensor_copy(w1_hi[:, e, :], w1_sb[:, e, :]).then_inc(w1_hi_ready, 1)
                pool.wait_ge(w1_hi_ready, e + 1)
                pool.tensor_tensor(w1_lo[:, e, :], w1_sb[:, e, :], w1_hi[:, e, :].bitcast(F32), ALU.subtract) \
                    .then_inc(w1_split, 1)

            def scale_of(b):
                pool.wait_ge(var_ready, 2 * B + b + 1)
                pool.tensor_tensor(rstd[:, b, 0:QT], var_eps[:, b, 0:QT], half_power[:, 0:QT], ALU.pow) \
                    .then_inc(rstd_ready, 1)

            pool.wait_ge(w1_loaded, 16)
            for e in range(5):
                split_w1(e)
            scale_of(0)
            for e in range(5, E):
                split_w1(e)
            scale_of(1)


_INS = ['x', 'ctx_1024', 'L0_xattn_ln_m_g', 'L0_xattn_ln_m_b', 'L0_xattn_ln_l_g', 'L0_xattn_ln_l_b',
        'L0_xattn_Wq', 'L0_xattn_Wkv', 'L0_xattn_Wout', 'L0_ffn_Wg', 'L0_ffn_W1', 'L0_ffn_b1',
        'L0_ffn_W2', 'L0_ffn_b2']


def kernel(**inputs):
    import numpy as _np
    import concourse.bacc as _bacc
    from concourse import mybir as _mybir
    from concourse.bass_utils import run_bass_kernel_spmd as _run

    nc = _bacc.Bacc("TRN2", target_bir_lowering=False, num_devices=1)
    arrays, args = {}, []
    for name in _INS:
        a = _np.ascontiguousarray(inputs[name])
        arrays[f"in_{name}"] = a
        args.append(nc.dram_tensor(f"in_{name}", a.shape, _mybir.dt.from_np(a.dtype), kind="ExternalInput").ap())
    out = nc.dram_tensor("out_0", (B, N, D), _mybir.dt.float32, kind="ExternalOutput").ap()
    xattn_moe(nc, *args, out)
    r = _run(nc, [arrays], core_ids=[0])
    return r.results[0]["out_0"]
```

```python
from contextlib import ExitStack

import concourse.bass as bass
from concourse import mybir

F32 = mybir.dt.float32
F32R = mybir.dt.float32r
ALU = mybir.AluOpType
ACT = mybir.ActivationFunctionType
AX = mybir.AxisListType

P = 128
B, N, D = 2, 512, 128
M = 154
H, HD = 16, 64
PAIRS = H // 2
STEPS = PAIRS * B
J = N + M
JP = J + 2
JH = J // 2
QT = N // P
KT = 6
KP = J // KT
TILES = 2 * QT
CT = 2
CP = M // CT
E, HID, TOPK = 8, 256, 2
HC = HID // P
EPS = 1e-5
SCALE = HD ** -0.5

TURN_A = {n: 2 * n - 3 for n in range(2, TILES)}
PVS = {n: n - 4 for n in range(4, TILES)}
PVS_LATE = {0: KT - 2, 1: KT - 1}
UNITS = {0: "Q", 2: "K0", 4: "K1", 6: "V0", 7: "V1"}
TURN_B = {n: 2 * n - 2 for n in range(1, TILES - 1)}
O_COPY = 2
SPLIT_V = 7
SPLIT_QK = 6
RING = 6


def unit_of(beat, last):
    kind = UNITS.get(beat)
    return None if last and kind and kind[0] in "QK" else kind


def xattn_moe(nc, x, ctx_in, g_m, b_m, g_l, b_l, wq, wkv, wout, wg, w1, b1, w2, b2, out):
    with ExitStack() as stack:
        def sb(name, shape, dt=F32):
            return stack.enter_context(nc.sbuf_tensor(name, shape, dt))

        def ps(name, shape):
            return stack.enter_context(nc.psum_tensor(name, shape, F32))

        def sem(name):
            return stack.enter_context(nc.semaphore(name))

        x_tok = sb("x_tok", [P, B, QT, D])
        ctx_tok = sb("ctx_tok", [CP, B, CT, D])
        rows = sb("rows", [E * HC + 4, P])
        cols = sb("cols", [P, E * HC + 4])
        ident = sb("ident", [P, P])
        earlier = sb("earlier", [P, E, E])
        half_power = sb("half_power", [P, QT + CT])
        stats = sb("stats", [P, B, QT + CT, 6])
        moments = sb("moments", [P, B, QT + CT, 2])
        var_eps = sb("var_eps", [P, B, QT + CT])
        rstd = sb("rstd", [P, B, QT + CT])
        normed = sb("normed", [P, B, QT + CT, D])
        kv_t = sb("kv_t", [P, B, JP])
        kv_hi = sb("kv_hi", [P, B, JP], F32R)
        kv_lo = sb("kv_lo", [P, B, JP], F32R)
        wqk_raw = sb("wqk_raw", [P, 2, P])
        wqk_hi = sb("wqk_hi", [P, 2, P], F32R)
        wqk_lo = sb("wqk_lo", [P, 2, P], F32R)
        wv_raw = sb("wv_raw", [P, P])
        wv_hi = sb("wv_hi", [P, P], F32R)
        wv_lo = sb("wv_lo", [P, P], F32R)
        q_st = sb("q_st", [P, B, 2, 2, N], F32R)
        k_pair = sb("k_pair", [P, 2, JP], F32R)
        k_st = sb("k_st", [P, B, 2, JP], F32R)
        v_sb = sb("v_sb", [P, B, KT, P])
        neg_max = sb("neg_max", [P, B, TILES])
        sums = sb("sums", [P, B, TILES])
        recips = sb("recips", [P, B, TILES])
        probs = sb("probs", [P, B, TILES, J])
        ring = sb("ring", [P, RING, N])
        o_t = sb("o_t", [P, B, PAIRS, N])
        wout_sb = sb("wout_sb", [P, PAIRS, D])
        w1_sb = sb("w1_sb", [P, E, HID])
        w1_hi = sb("w1_hi", [P, E, HID], F32R)
        w1_lo = sb("w1_lo", [P, E, HID], F32R)
        w2_sb = sb("w2_sb", [P, E * HC, D])
        wg_sb = sb("wg_sb", [P, E])
        b2_sb = sb("b2_sb", [E, D])
        acc = sb("acc", [P, B, QT, D])
        g_neg = sb("g_neg", [P, B, QT])
        g_sub = sb("g_sub", [P, B, QT, E])
        g_exp = sb("g_exp", [P, B, QT, E])
        g_sum = sb("g_sum", [P, B, QT])
        g_rec = sb("g_rec", [P, B, QT])
        g_prob = sb("g_prob", [P, B, QT, E])
        g_gt = sb("g_gt", [P, B, QT, E, E])
        g_eq = sb("g_eq", [P, B, QT, E, E])
        g_rank = sb("g_rank", [P, B, QT, E])
        g_top = sb("g_top", [P, B, QT, E])
        g_tsum = sb("g_tsum", [P, B, QT])
        g_trec = sb("g_trec", [P, B, QT])
        score = sb("score", [P, B, QT, E])
        score_t = sb("score_t", [E, B, N])

        slots = ps("slots", [P, 2, 2, N])
        turned = ps("turned", [P, 2, N])
        proj = ps("proj", [P, N])
        o_ps = ps("o_ps", [P, N])
        first_k = [slots[:, 0, half, :] for half in range(2)]
        hid_ps = slots[:, :, :, :].rearrange("p a b n -> p (a b) n")

        x_in = [sem(f"x_in{b}") for b in range(B)]
        ctx_loaded = sem("ctx_loaded")
        rows_loaded = sem("rows_loaded")
        wqk_loaded = sem("wqk_loaded")
        wv_loaded = sem("wv_loaded")
        w1_loaded = sem("w1_loaded")
        tail_loaded = sem("tail_loaded")
        consts = sem("consts")
        cols_turned = sem("cols_turned")
        cols_ready = sem("cols_ready")
        setup_p = sem("setup_p")
        setup_v = sem("setup_v")
        var_ready = sem("var_ready")
        rstd_ready = sem("rstd_ready")
        normed_ready = sem("normed_ready")
        normed1_ready = sem("normed1_ready")
        norm_turned = sem("norm_turned")
        kv_ready = sem("kv_ready")
        kv_hi_ready = sem("kv_hi_ready")
        kv_lo_ready = sem("kv_lo_ready")
        wqk_hi_ready = sem("wqk_hi_ready")
        wqk_split = sem("wqk_split")
        wv_hi_ready = sem("wv_hi_ready")
        wv_split = sem("wv_split")
        scores_ready = sem("scores_ready")
        q_ready = sem("q_ready")
        k_ready = sem("k_ready")
        v_ready = sem("v_ready")
        max_done = sem("max_done")
        exp_done = sem("exp_done")
        recip_done = sem("recip_done")
        prob_done = sem("prob_done")
        q_hi_done = sem("q_hi_done")
        q_lo_done = sem("q_lo_done")
        spread_done = [[sem(f"spread_done{b}{h}") for h in range(2)] for b in range(B)]
        k_hi_done = sem("k_hi_done")
        k_lo_done = sem("k_lo_done")
        v_copied = sem("v_copied")
        turn_ready = sem("turn_ready")
        even_copied = sem("even_copied")
        odd_copied = sem("odd_copied")
        pv_done = sem("pv_done")
        o_copied = sem("o_copied")
        out_proj = sem("out_proj")
        x1_ready = sem("x1_ready")
        w1_split = sem("w1_split")
        w1_hi_ready = sem("w1_hi_ready")
        x2_turned = sem("x2_turned")
        x2_copied = sem("x2_copied")
        x2_hi = sem("x2_hi")
        x2_lo = sem("x2_lo")
        logits_ready = sem("logits_ready")
        gate_sub = sem("gate_sub")
        gate_exp = sem("gate_exp")
        gate_v = sem("gate_v")
        score_ready = sem("score_ready")
        score_turned = sem("score_turned")
        score_copied = sem("score_copied")
        bias_ready = sem("bias_ready")
        acc_ready = sem("acc_ready")
        hid_ready = sem("hid_ready")
        relu_done = sem("relu_done")
        y_ready = sem("y_ready")
        acc_v = sem("acc_v")
        stored = sem("stored")

        block = stack.enter_context(nc.Block())

        wq_pair = wq.rearrange("d (r c) -> d r c", c=P)
        wkv_pair = wkv.rearrange("d (r c) -> d r c", c=P)

        def in_step(run):
            def for_engine(eng):
                for b in range(B):
                    run(0, b, b, b, False)
                with eng.Fori(1, PAIRS - 1) as pair:
                    for b in range(B):
                        run(pair, b, 2 * pair + b, B, False)
                for b in range(B):
                    run(PAIRS - 1, b, 2 * (PAIRS - 1) + b, B, b == B - 1)
            return for_engine

        @block.sync
        def _(sp):
            for b in range(B):
                sp.dma_start(x_tok[:, b], x[b].rearrange("(t p) d -> p t d", p=P)).then_inc(x_in[b], 16)
                if b == 0:
                    sp.dma_start(ctx_tok[:, :, :, :].rearrange("p b t d -> p (b t) d"),
                                 ctx_in.rearrange("b (t p) d -> p (b t) d", p=CP)).then_inc(ctx_loaded, 16)
            sp.dma_start(rows[0:E * HC, :], b1.rearrange("e (c p) -> (e c) p", p=P)).then_inc(rows_loaded, 16)
            sp.dma_start(wv_raw[:, :], wkv_pair[:, PAIRS]).then_inc(wv_loaded, 16)
            def load_qk(pair):
                sp.wait_ge(wqk_split, pair)
                sp.dma_start(wqk_raw[:, 0], wq_pair[:, bass.ds(pair, 1)]).then_inc(wqk_loaded, 16)
                sp.dma_start(wqk_raw[:, 1], wkv_pair[:, bass.ds(pair, 1)]).then_inc(wqk_loaded, 16)

            def load_v(pair):
                sp.wait_ge(wv_split, pair)
                sp.dma_start(wv_raw[:, :], wkv_pair[:, bass.ds(pair + PAIRS, 1)]).then_inc(wv_loaded, 16)

            def double_q(b, h, step):
                sp.wait_ge(q_lo_done, 2 * step + h + 1)
                own, other = slice(h * HD, (h + 1) * HD), slice((1 - h) * HD, (2 - h) * HD)
                sp.dma_start(q_st[other, b, h].bitcast(F32), q_st[own, b, h].bitcast(F32)) \
                  .then_inc(spread_done[b][h], 16)

            def stack_k(b, h, step):
                sp.wait_ge(k_lo_done, 2 * (step + 1))
                for part in range(2):
                    sp.dma_start(k_st[part * HD:(part + 1) * HD, b, h, :].bitcast(F32),
                                 k_pair[h * HD:(h + 1) * HD, part, :].bitcast(F32)) \
                      .then_inc(spread_done[b][h], 16)

            def spread(b, step):
                for h in range(2):
                    double_q(b, h, step)
                for h in range(2):
                    stack_k(b, h, step)

            for h in range(2):
                stack_k(0, h, 0)
                double_q(0, h, 0)
            load_qk(1)
            sp.dma_start(w1_sb[:, :, :], w1.rearrange("e d h -> d e h")).then_inc(w1_loaded, 16)
            sp.dma_start(wout_sb[:, :, :], wout.rearrange("(r p) d -> p r d", p=P)).then_inc(tail_loaded, 16)
            sp.dma_start(w2_sb[:, :, :], w2.rearrange("e (c p) d -> p (e c) d", p=P)).then_inc(tail_loaded, 16)
            sp.dma_start(wg_sb[:, :], wg).then_inc(tail_loaded, 16)
            sp.dma_start(b2_sb[:, :], b2).then_inc(tail_loaded, 16)
            spread(1, 1)
            load_v(1)
            with sp.Fori(1, PAIRS - 1) as pair:
                spread(0, 2 * pair)
                load_qk(pair + 1)
                spread(1, 2 * pair + 1)
                load_v(pair + 1)
            spread(0, STEPS - 2)
            spread(1, STEPS - 1)
            for b in range(B):
                sp.wait_ge(acc_v, QT * E * (b + 1))
                sp.dma_start(out[b].rearrange("(t p) d -> p t d", p=P), acc[:, b]).then_inc(stored, 16)
            sp.wait_ge(stored, 16 * B)

        @block.tensor
        def _(pe):
            def three(out_ap, st_hi, st_lo, mv_hi, mv_lo):
                pe.matmul(out_ap, st_hi, mv_hi, start=True, stop=False)
                pe.matmul(out_ap, st_hi, mv_lo, start=False, stop=False)
                return pe.matmul(out_ap, st_lo, mv_hi, start=False, stop=True)

            def scores(pair, b, step, n, first):
                h, t, slot = n // QT, n % QT, n % 2
                if n < 2:
                    if first:
                        pe.wait_ge(exp_done, TILES * (step - 1) + n + 7)
                else:
                    pe.wait_ge(exp_done, TILES * step + n - 1)
                if n == 1 and not first:
                    pe.wait_ge(kv_lo_ready, 2 * B)
                if t == 0:
                    pe.wait_ge(spread_done[b][h], 48 * (pair + 1))
                for part in range(2):
                    for half in range(2):
                        mm = pe.matmul(slots[:, slot, half, 0:JH + 1], q_st[:, b, h, part, t * P:(t + 1) * P],
                                       k_st[:, b, h, half * JH:half * JH + JH + 1],
                                       start=(part == 0), stop=(part == 1))
                mm.then_inc(scores_ready, 1)

            def project_q(b):
                three(proj[:, :], wqk_hi[:, 0, :], wqk_lo[:, 0, :], kv_hi[:, b, 0:N], kv_lo[:, b, 0:N]) \
                    .then_inc(q_ready, 1)

            def project_k(b, half, bank=proj):
                at = slice(half * JP // 2, (half + 1) * JP // 2)
                three(bank[:, 0:JP // 2], wqk_hi[:, 1, :], wqk_lo[:, 1, :], kv_hi[:, b, at], kv_lo[:, b, at]) \
                    .then_inc(k_ready, 1)

            def project_v(b, half):
                for k in range(KT // 2):
                    kt = half * KT // 2 + k
                    at = slice(kt * KP, (kt + 1) * KP)
                    mm = three(proj[0:KP, k * P:(k + 1) * P], kv_hi[:, b, at], kv_lo[:, b, at],
                               wv_hi[:, :], wv_lo[:, :])
                mm.then_inc(v_ready, 1)

            def project(pair, b, step, first, last, kind):
                if kind == "Q":
                    if first == 0 and b == 0:
                        pe.wait_ge(kv_lo_ready, 2 * B)
                        pe.wait_ge(q_lo_done, 2)
                    else:
                        pe.wait_ge(v_copied, 2 * step)
                    pe.wait_ge(wqk_split, pair + b + 1)
                    project_q(1 - b)
                elif kind == "K0":
                    pe.wait_ge(q_lo_done, 2 * (step + 2))
                    project_k(1 - b, 0)
                elif kind == "K1":
                    pe.wait_ge(k_lo_done, 2 * (step + 2) - 1)
                    project_k(1 - b, 1)
                elif kind == "V0":
                    if last:
                        pe.wait_ge(v_copied, 2 * step)
                    else:
                        pe.wait_ge(k_lo_done, 2 * (step + 2))
                    pe.wait_ge(wv_split, pair + 1)
                    project_v(b, 0)
                else:
                    pe.wait_ge(v_copied, 2 * step + 1)
                    project_v(b, 1)

            def turn(b, of, i, no_earlier=False):
                kt, h = i // 2, i % 2
                if i < 2:
                    pe.wait_ge(prob_done, TILES * of + QT * (h + 1))
                g = i - 2
                if g >= 0 or not no_earlier:
                    pe.wait_ge(even_copied if g % 2 == 0 else odd_copied, 6 * of + g // 2 + 1)
                for t in range(QT):
                    mm = pe.transpose(turned[0:KP, i % 2, t * P:(t + 1) * P],
                                      probs[:, b, h * QT + t, kt * KP:(kt + 1) * KP], ident[:, :])
                mm.then_inc(turn_ready, 1)

            def pv(b, of, kt, no_earlier=False):
                if kt == 0:
                    pe.wait_ge(v_copied, 2 * (of + 1))
                    if not no_earlier:
                        pe.wait_ge(o_copied, of)
                pe.wait_ge(even_copied, 6 * of + kt + 1)
                pe.wait_ge(odd_copied, 6 * of + kt + 1)
                for h in range(2):
                    mm = pe.matmul(o_ps[h * HD:(h + 1) * HD, :], v_sb[0:KP, b, kt, h * HD:(h + 1) * HD],
                                   ring[0:KP, (2 * kt + h) % RING, :], start=(kt == 0), stop=(kt == KT - 1))
                mm.then_inc(pv_done, 1)

            pe.wait_ge(consts, 1)
            pe.wait_ge(rows_loaded, 16 * 5)
            pe.transpose(o_ps[:, 0:E * HC + 4], rows[:, :], ident[0:E * HC + 4, 0:E * HC + 4]) \
              .then_inc(cols_turned, 1)
            def turn_inputs(b, bank):
                for t in range(QT):
                    pe.transpose(bank[:, 0, t * P:(t + 1) * P], normed[:, b, t, :], ident[:, :])
                for t in range(CT):
                    mm = pe.transpose(bank[:, 1, t * CP:(t + 1) * CP], normed[0:CP, b, QT + t, :],
                                      ident[0:CP, 0:CP])
                mm.then_inc(norm_turned, 1)

            pe.wait_ge(normed_ready, QT + CT)
            turn_inputs(0, turned)
            pe.wait_ge(kv_lo_ready, 1)
            pe.wait_ge(wqk_split, 1)
            project_k(0, 0, first_k[0])
            pe.wait_ge(kv_lo_ready, 2)
            project_k(0, 1, first_k[1])
            project_q(0)
            pe.wait_ge(normed1_ready, QT + CT)
            turn_inputs(1, slots[:, 1])

            def run(pair, b, step, first, last):
                for n in range(TILES):
                    scores(pair, b, step, n, first)
                    if first >= 1 and n in TURN_A:
                        turn(1 - b, step - 1, TURN_A[n], no_earlier=(first == 1))
                    if n in PVS_LATE and first >= 2:
                        pv(b, step - 2, PVS_LATE[n])
                    if first >= 1 and n in PVS:
                        pv(1 - b, step - 1, PVS[n], no_earlier=(first == 1))
                    if unit_of(n, last):
                        project(pair, b, step, first, last, unit_of(n, last))
                    if first >= 1 and n in TURN_B:
                        turn(1 - b, step - 1, TURN_B[n], no_earlier=(first == 1))

            in_step(run)(pe)

            def out_project(b, bank):
                for t in range(QT):
                    for r in range(PAIRS):
                        mm = pe.matmul(bank[:, t * P:(t + 1) * P], o_t[:, b, r, t * P:(t + 1) * P],
                                       wout_sb[:, r, :], start=(r == 0), stop=(r == PAIRS - 1))
                mm.then_inc(out_proj, 1)

            def turn_x2(b):
                pe.wait_ge(normed_ready, QT + CT + QT * (b + 1))
                if b:
                    pe.wait_ge(acc_ready, 1)
                for t in range(QT):
                    mm = pe.transpose(proj[:, t * P:(t + 1) * P], normed[:, b, t, :], ident[:, :])
                mm.then_inc(x2_turned, 1)

            def logits(b):
                pe.wait_ge(x2_copied, b + 1)
                pe.wait_ge(o_copied, STEPS) if b == 0 else pe.wait_ge(score_copied, 1)
                for t in range(QT):
                    mm = pe.matmul(o_ps[:, t * E:(t + 1) * E], kv_t[:, b, t * P:(t + 1) * P], wg_sb[:, :],
                                   start=True, stop=True)
                mm.then_inc(logits_ready, 1)

            def bias_term(b):
                pe.wait_ge(score_ready, b + 1)
                for t in range(QT):
                    mm = pe.transpose(o_ps[0:E, t * P:(t + 1) * P], score[:, b, t, :], ident[:, :])
                mm.then_inc(score_turned, 1)
                pe.wait_ge(score_copied, b + 1)
                pe.wait_ge(x2_lo, b + 1)
                for t in range(QT):
                    mm = pe.matmul(proj[:, t * P:(t + 1) * P], score_t[:, b, t * P:(t + 1) * P],
                                   b2_sb[:, :], start=True, stop=True)
                mm.then_inc(bias_ready, 1)

            def hidden(g):
                b, e = g // E, g % E
                if g == 0:
                    pe.wait_ge(x1_ready, B)
                if e == 0:
                    pe.wait_ge(x2_lo, b + 1)
                pe.wait_ge(w1_split, min(g + 1, E))
                for c in range(HC):
                    n = g * HC + c
                    if n >= 4:
                        pe.wait_ge(relu_done, n - 3)
                    three(hid_ps[:, n % 4, :], w1_hi[:, e, c * P:(c + 1) * P], w1_lo[:, e, c * P:(c + 1) * P],
                          kv_hi[:, b, 0:N], kv_lo[:, b, 0:N]).then_inc(hid_ready, 1)

            def expert_out(g):
                e = g % E
                if g >= 2:
                    pe.wait_ge(acc_v, QT * (g - 1))
                elif g == 0:
                    pe.wait_ge(odd_copied, 6 * STEPS)
                pe.wait_ge(relu_done, HC * (g + 1))
                for t in range(QT):
                    for c in range(HC):
                        mm = pe.matmul(turned[:, g % 2, t * P:(t + 1) * P],
                                       ring[:, (g * HC + c) % RING, t * P:(t + 1) * P],
                                       w2_sb[:, e * HC + c, :], start=(c == 0), stop=(c == HC - 1))
                mm.then_inc(y_ready, 1)

            pv(0, STEPS - 2, KT - 2)
            pv(0, STEPS - 2, KT - 1)
            pe.wait_ge(tail_loaded, 16 * 4)
            pe.wait_ge(o_copied, STEPS - 1)
            pe.wait_ge(exp_done, TILES * STEPS)
            out_project(0, slots[:, 0, 0, :])
            for i in range(2 * KT):
                turn(1, STEPS - 1, i)
                if i >= 3 and i % 2 == 1:
                    pv(1, STEPS - 1, i // 2 - 1)
            pv(1, STEPS - 1, KT - 1)
            turn_x2(0)
            pe.wait_ge(o_copied, STEPS)
            out_project(1, slots[:, 1, 0, :])
            logits(0)
            for g in range(B * E):
                hidden(g)
                if g % E == 1:
                    bias_term(g // E)
                if g >= 1:
                    expert_out(g - 1)
                if g == E // 2:
                    turn_x2(1)
                if g == E // 2 + 1:
                    logits(1)
            expert_out(B * E - 1)

        @block.scalar
        def _(act):
            act.dma_start(wqk_raw[:, 1], wkv_pair[:, 0]).then_inc(wqk_loaded, 16)
            act.dma_start(wqk_raw[:, 0], wq_pair[:, 0]).then_inc(wqk_loaded, 16)
            for n, v in enumerate([g_l, b_l, g_m, b_m]):
                act.dma_start(rows[E * HC + n:E * HC + n + 1, :], v.rearrange("(a d) -> a d", a=1)) \
                   .then_inc(rows_loaded, 16)
            def split_qk(n):
                act.wait_ge(wqk_loaded, 32 * (n + 1))
                act.copy(wqk_hi[:, :, :], wqk_raw[:, :, :]).then_inc(wqk_hi_ready, 1)

            def split_v(n):
                act.wait_ge(wv_loaded, 16 * (n + 1))
                act.copy(wv_hi[:, :], wv_raw[:, :]).then_inc(wv_hi_ready, 1)

            def q_high(b, step):
                act.wait_ge(q_ready, step + 1)
                for h in range(2):
                    own = slice(h * HD, (h + 1) * HD)
                    act.activation(q_st[own, b, h, 0, :], proj[own, :], ACT.Copy, scale=SCALE) \
                       .then_inc(q_hi_done, 1)

            def k_high(step, half, before=None, bank=proj):
                act.wait_ge(k_ready, 2 * step + half + 1)
                if half == 0 and before:
                    pair, b = before
                    for h in range(2):
                        act.wait_ge(spread_done[b][h], 48 * (pair + 1))
                at = slice(half * JP // 2, (half + 1) * JP // 2)
                act.copy(k_pair[:, 0, at], bank[:, 0:JP // 2]).then_inc(k_hi_done, 1)

            def copy_v(b, step, half):
                act.wait_ge(v_ready, 2 * step + half + 1)
                kts = slice(half * KT // 2, (half + 1) * KT // 2)
                act.copy(v_sb[0:KP, b, kts].rearrange("p k c -> p (k c)"), proj[0:KP, 0:KT // 2 * P]) \
                   .then_inc(v_copied, 1)

            def copy_turned(of, i, no_earlier):
                act.wait_ge(turn_ready, 2 * KT * of + i + 1)
                if not (no_earlier and i < RING):
                    act.wait_ge(pv_done, KT * of + (i - RING) // 2 + 1)
                act.copy(ring[0:KP, i % RING, :], turned[0:KP, i % 2, :]).then_inc(even_copied, 1)

            act.wait_ge(cols_turned, 1)
            act.copy(cols[:, :], o_ps[:, 0:E * HC + 4]).then_inc(cols_ready, 1)
            split_qk(0)
            split_v(0)
            def inputs_high(b):
                for i, at in enumerate([slice(0, N), slice(N, JP)]):
                    act.wait_ge(kv_ready, 2 * b + i + 2)
                    act.copy(kv_hi[:, b, at], kv_t[:, b, at]).then_inc(kv_hi_ready, 1)

            inputs_high(0)
            k_high(0, 0, bank=first_k[0])
            k_high(0, 1, bank=first_k[1])
            q_high(0, 0)
            inputs_high(1)

            def run(pair, b, step, first, last):
                for n in range(TILES):
                    kind = unit_of(n, last)
                    act.wait_ge(max_done, TILES * step + n + 1)
                    act.activation(probs[:, b, n, :].rearrange("p (a n) -> p a n", a=2),
                                   slots[:, n % 2, :, 0:JH], ACT.Exp, bias=neg_max[:, b, n:n + 1],
                                   accum_out=sums[:, b, n:n + 1]).then_inc(exp_done, 1)
                    if kind == "Q":
                        q_high(1 - b, step + 1)
                    elif kind and kind[0] == "K":
                        k_high(step + 1, int(kind[1]), before=(pair, b))
                    elif kind:
                        copy_v(b, step, int(kind[1]))
                    if first >= 1 and n in TURN_B:
                        copy_turned(step - 1, TURN_B[n], first == 1)
                    if b == 1 and n == SPLIT_V and not last:
                        act.wait_ge(v_ready, 2 * (step + 1))
                        split_v(pair + 1)
                    if b == 0 and n == SPLIT_QK and not (first == B and isinstance(pair, int)):
                        act.wait_ge(k_ready, 2 * (step + 2))
                        split_qk(pair + 1)

            in_step(run)(act)
            for i in range(0, 2 * KT, 2):
                copy_turned(STEPS - 1, i, False)

            def gate_exp_of(b):
                act.wait_ge(gate_sub, b + 1)
                act.activation(g_exp[:, b], g_sub[:, b], ACT.Exp).then_inc(gate_exp, 1)

            def copy_x2(b):
                act.wait_ge(x2_turned, b + 1)
                act.copy(kv_t[:, b, 0:N], proj[:, :]).then_inc(x2_copied, 1)
                act.copy(kv_hi[:, b, 0:N], proj[:, :]).then_inc(x2_hi, 1)

            def relu(n):
                act.wait_ge(hid_ready, n + 1)
                if n >= RING:
                    act.wait_ge(y_ready, (n - RING) // HC + 1)
                act.activation(ring[:, n % RING, :], hid_ps[:, n % 4, :], ACT.Relu,
                               bias=cols[:, n % (E * HC):n % (E * HC) + 1]).then_inc(relu_done, 1)

            def copy_scores(b):
                act.wait_ge(score_turned, b + 1)
                act.copy(score_t[:, b, :], o_ps[0:E, :]).then_inc(score_copied, 1)

            act.wait_ge(pv_done, KT * STEPS)
            copy_x2(0)
            gate_exp_of(0)
            for g in range(B * E):
                for c in range(HC):
                    relu(g * HC + c)
                if g % E == 1:
                    copy_scores(g // E)
                if g == E // 2:
                    copy_x2(1)
                if g == E // 2 + 1:
                    gate_exp_of(1)

        @block.vector
        def _(dve):
            own = [0]

            def chained(op):
                op.then_inc(setup_v, 1)
                own[0] += 1
                dve.wait_ge(setup_v, own[0])

            def moments_of(b, tiles):
                for n, tile in tiles:
                    ins = dve.bn_stats(stats[0:tile.shape[0], b, n, :], tile)
                chained(ins)
                for n, tile in tiles:
                    ins = dve.bn_aggr(moments[0:tile.shape[0], b, n, :], stats[0:tile.shape[0], b, n, :])
                chained(ins)

            def apply_norm(b, tiles):
                for n, tile in tiles:
                    r = tile.shape[0]
                    dve.tensor_scalar(normed[0:r, b, n, :], tile, moments[0:r, b, n, 0:1],
                                      rstd[0:r, b, n:n + 1], ALU.subtract, ALU.mult).then_inc(normed_ready, 1)

            def q_low(b, step):
                for h in range(2):
                    own = slice(h * HD, (h + 1) * HD)
                    dve.wait_ge(q_hi_done, 2 * step + h + 1)
                    dve.scalar_tensor_tensor(q_st[own, b, h, 1, :], proj[own, :], SCALE,
                                             q_st[own, b, h, 0, :].bitcast(F32), ALU.mult, ALU.subtract) \
                       .then_inc(q_lo_done, 1)

            def k_low(step, half, before=None, bank=proj):
                dve.wait_ge(k_hi_done, 2 * step + half + 1)
                if half == 0 and before:
                    pair, b = before
                    for h in range(2):
                        dve.wait_ge(spread_done[b][h], 48 * (pair + 1))
                at = slice(half * JP // 2, (half + 1) * JP // 2)
                dve.tensor_tensor(k_pair[:, 1, at], bank[:, 0:JP // 2], k_pair[:, 0, at].bitcast(F32),
                                  ALU.subtract).then_inc(k_lo_done, 1)

            chained(dve.memset(moments[:, :, :, :], 1.0))
            dve.memset(kv_t[:, :, J:JP], 0.0).then_inc(kv_ready, 1)
            def input_tiles(b):
                return [(t, x_tok[:, b, t, :]) for t in range(QT)] + \
                       [(QT + t, ctx_tok[:, b, t, :]) for t in range(CT)]

            for b in range(B):
                dve.wait_ge(x_in[b], 16)
                dve.wait_ge(ctx_loaded, 16)
                moments_of(b, input_tiles(b))
                dve.tensor_scalar(var_eps[:, b, 0:QT], moments[:, b, 0:QT, 1], 1.0 + EPS, EPS * EPS,
                                  ALU.mult, ALU.add).then_inc(var_ready, 1)
                dve.tensor_scalar(var_eps[:, b, QT:QT + CT], moments[:, b, QT:QT + CT, 1], EPS, None,
                                  ALU.add).then_inc(var_ready, 1)
            dve.wait_ge(rstd_ready, 1)
            apply_norm(0, input_tiles(0))
            dve.wait_ge(wqk_hi_ready, 1)
            dve.tensor_tensor(wqk_lo[:, :, :], wqk_raw[:, :, :], wqk_hi[:, :, :].bitcast(F32),
                              ALU.subtract).then_inc(wqk_split, 1)
            dve.wait_ge(wv_hi_ready, 1)
            dve.tensor_tensor(wv_lo[:, :], wv_raw[:, :], wv_hi[:, :].bitcast(F32),
                              ALU.subtract).then_inc(wv_split, 1)

            def inputs_low(b, bank):
                dve.wait_ge(norm_turned, b + 1)
                g = E * HC
                dve.tensor_scalar(kv_t[:, b, 0:N], bank[:, 0, :], cols[:, g:g + 1], cols[:, g + 1:g + 2],
                                  ALU.mult, ALU.add).then_inc(kv_ready, 1)
                dve.tensor_scalar(kv_t[:, b, N:J], bank[:, 1, 0:M], cols[:, g + 2:g + 3],
                                  cols[:, g + 3:g + 4], ALU.mult, ALU.add).then_inc(kv_ready, 1)
                for i, at in enumerate([slice(0, N), slice(N, JP)]):
                    dve.wait_ge(kv_hi_ready, 2 * b + i + 1)
                    dve.tensor_tensor(kv_lo[:, b, at], kv_t[:, b, at], kv_hi[:, b, at].bitcast(F32),
                                      ALU.subtract).then_inc(kv_lo_ready, 1)

            dve.wait_ge(cols_ready, 1)
            inputs_low(0, turned)
            k_low(0, 0, bank=first_k[0])
            k_low(0, 1, bank=first_k[1])
            q_low(0, 0)
            inputs_low(1, slots[:, 1])

            def copy_turned(of, i, no_earlier):
                dve.wait_ge(turn_ready, 2 * KT * of + i + 1)
                if not (no_earlier and i < RING):
                    dve.wait_ge(pv_done, KT * of + (i - RING) // 2 + 1)
                dve.tensor_copy(ring[0:KP, i % RING, :], turned[0:KP, i % 2, :]).then_inc(odd_copied, 1)

            def reciprocal(b, step, n):
                dve.wait_ge(exp_done, TILES * step + n + 1)
                dve.reciprocal(recips[:, b, n:n + 1], sums[:, b, n:n + 1]).then_inc(recip_done, 1)

            def copy_output(b, of, pair):
                dve.wait_ge(pv_done, KT * (of + 1))
                if isinstance(pair, int):
                    to = o_t[:, b, pair, :]
                else:
                    to = o_t[:, b, bass.ds(pair, 1), :].rearrange("p a n -> p (a n)")
                dve.tensor_copy(to, o_ps[:, :]).then_inc(o_copied, 1)

            def run(pair, b, step, first, last):
                for n in range(TILES):
                    kind = unit_of(n, last)
                    dve.wait_ge(scores_ready, TILES * step + n + 1)
                    dve.tensor_reduce(neg_max[:, b, n:n + 1], slots[:, n % 2, :, 0:JH], AX.XY, ALU.max,
                                      negate=True).then_inc(max_done, 1)
                    if first >= 1 and n in TURN_A:
                        copy_turned(step - 1, TURN_A[n], first == 1)
                    if n >= 1:
                        reciprocal(b, step, n - 1)
                    elif first >= 1:
                        reciprocal(1 - b, step - 1, TILES - 1)
                    before = unit_of(n - 1, last)
                    if before == "Q":
                        q_low(1 - b, step + 1)
                    elif before and before[0] == "K":
                        k_low(step + 1, int(before[1]), before=(pair, b))
                    if n == O_COPY and first >= 2:
                        copy_output(b, step - 2, pair - 1)
                    if b == 1 and n == SPLIT_V and not last:
                        dve.wait_ge(wv_hi_ready, pair + 2)
                        dve.tensor_tensor(wv_lo[:, :], wv_raw[:, :], wv_hi[:, :].bitcast(F32),
                                          ALU.subtract).then_inc(wv_split, 1)
                    if b == 0 and n == SPLIT_QK and not (first == B and isinstance(pair, int)):
                        dve.wait_ge(wqk_hi_ready, pair + 2)
                        dve.tensor_tensor(wqk_lo[:, :, :], wqk_raw[:, :, :], wqk_hi[:, :, :].bitcast(F32),
                                          ALU.subtract).then_inc(wqk_split, 1)

            in_step(run)(dve)
            reciprocal(1, STEPS - 1, TILES - 1)
            copy_output(0, STEPS - 2, PAIRS - 1)

            def x1_and_moments(b, bank):
                dve.wait_ge(out_proj, b + 1)
                dve.tensor_tensor(acc[:, b].rearrange("p t d -> p (t d)"), bank,
                                  x_tok[:, b].rearrange("p t d -> p (t d)"), ALU.add).then_inc(x1_ready, 1)
                dve.wait_ge(x1_ready, b + 1)
                moments_of(b, [(t, acc[:, b, t, :]) for t in range(QT)])
                dve.tensor_scalar(var_eps[:, b, 0:QT], moments[:, b, 0:QT, 1], EPS, None, ALU.add) \
                   .then_inc(var_ready, 1)

            def norm_x1(b):
                dve.wait_ge(rstd_ready, B + b + 1)
                apply_norm(b, [(t, acc[:, b, t, :]) for t in range(QT)])

            def split_x2(b):
                dve.wait_ge(x2_hi, b + 1)
                dve.tensor_tensor(kv_lo[:, b, 0:N], proj[:, :], kv_hi[:, b, 0:N].bitcast(F32),
                                  ALU.subtract).then_inc(x2_lo, 1)

            def gate_start(b):
                dve.wait_ge(logits_ready, b + 1)
                lg = o_ps[:, 0:QT * E].rearrange("p (t e) -> p t e", e=E)
                chained(dve.tensor_reduce(g_neg[:, b, :], lg, AX.X, ALU.max))
                dve.tensor_tensor(g_sub[:, b], lg, g_neg[:, b, :].unsqueeze(2).to_broadcast([P, QT, E]),
                                  ALU.subtract).then_inc(gate_sub, 1)

            def gate_end(b):
                dve.wait_ge(gate_exp, b + 1)
                chained(dve.tensor_reduce(g_sum[:, b, :], g_exp[:, b], AX.X, ALU.add))
                chained(dve.reciprocal(g_rec[:, b, :], g_sum[:, b, :]))
                chained(dve.tensor_tensor(g_prob[:, b], g_exp[:, b],
                                          g_rec[:, b, :].unsqueeze(2).to_broadcast([P, QT, E]), ALU.mult))
                for t in range(QT):
                    pj = g_prob[:, b, t, :].unsqueeze(1).to_broadcast([P, E, E])
                    pe_ = g_prob[:, b, t, :].unsqueeze(2).to_broadcast([P, E, E])
                    dve.tensor_tensor(g_gt[:, b, t], pj, pe_, ALU.is_gt)
                    ins = dve.tensor_tensor(g_eq[:, b, t], pj, pe_, ALU.is_equal)
                chained(ins)
                first_of = earlier[:, :, :].unsqueeze(1).to_broadcast([P, QT, E, E])
                chained(dve.tensor_tensor(g_eq[:, b], g_eq[:, b], first_of, ALU.mult))
                chained(dve.tensor_tensor(g_gt[:, b], g_gt[:, b], g_eq[:, b], ALU.add))
                chained(dve.tensor_reduce(g_rank[:, b], g_gt[:, b], AX.X, ALU.add))
                chained(dve.scalar_tensor_tensor(g_top[:, b], g_rank[:, b], float(TOPK), g_prob[:, b],
                                                 ALU.is_lt, ALU.mult))
                chained(dve.tensor_reduce(g_tsum[:, b, :], g_top[:, b], AX.X, ALU.add))
                chained(dve.reciprocal(g_trec[:, b, :], g_tsum[:, b, :]))
                dve.tensor_tensor(score[:, b], g_top[:, b],
                                  g_trec[:, b, :].unsqueeze(2).to_broadcast([P, QT, E]), ALU.mult) \
                   .then_inc(score_ready, 1)

            def add_bias(b):
                dve.wait_ge(bias_ready, b + 1)
                dve.tensor_tensor(acc[:, b].rearrange("p t d -> p (t d)"), proj[:, :],
                                  acc[:, b].rearrange("p t d -> p (t d)"), ALU.add).then_inc(acc_ready, 1)
                dve.wait_ge(acc_ready, b + 1)

            def add_expert(g):
                b, e = g // E, g % E
                dve.wait_ge(y_ready, g + 1)
                if e >= 1:
                    dve.wait_ge(acc_v, QT * g)
                for t in range(QT):
                    dve.scalar_tensor_tensor(acc[:, b, t, :], turned[:, g % 2, t * P:(t + 1) * P],
                                             score[:, b, t, e:e + 1], acc[:, b, t, :], ALU.mult, ALU.add) \
                       .then_inc(acc_v, 1)

            x1_and_moments(0, slots[:, 0, 0, :])
            copy_turned(STEPS - 1, 1, False)
            copy_turned(STEPS - 1, 3, False)
            norm_x1(0)
            for i in range(5, 2 * KT, 2):
                copy_turned(STEPS - 1, i, False)
            copy_output(1, STEPS - 1, PAIRS - 1)
            split_x2(0)
            x1_and_moments(1, slots[:, 1, 0, :])
            gate_start(0)
            norm_x1(1)
            gate_end(0)
            for g in range(B * E):
                if g % E == 0:
                    add_bias(g // E)
                add_expert(g)
                if g == E // 2 - 1:
                    split_x2(1)
                if g == E // 2:
                    gate_start(1)
                    gate_end(1)

        @block.gpsimd
        def _(pool):
            ones = pool.memset(ident[:, :], 0.0)
            ones.then_inc(setup_p, 1)
            pool.memset(earlier[:, :, :], 1.0).then_inc(setup_p, 1)
            pool.memset(half_power[:, :], -0.5).then_inc(setup_p, 1)
            pool.wait_ge(setup_p, 3)
            pool.affine_select(out=ident[:, :], in_=ident[:, :], compare_op=ALU.not_equal, fill=1.0,
                               base=0, pattern=[[-1, P]], channel_multiplier=1).then_inc(consts, 1)
            pool.affine_select(out=earlier[:, :, :], in_=earlier[:, :, :], compare_op=ALU.is_ge, fill=0.0,
                               base=-1, pattern=[[1, E], [-1, E]], channel_multiplier=0).then_inc(consts, 1)

            for b in range(B):
                pool.wait_ge(var_ready, 2 * (b + 1))
                pool.tensor_tensor(rstd[:, b, :], var_eps[:, b, :], half_power[:, :], ALU.pow) \
                    .then_inc(rstd_ready, 1)
            pool.wait_ge(rstd_ready, B)
            for n in range(QT + CT):
                tile = x_tok[:, 1, n, :] if n < QT else ctx_tok[:, 1, n - QT, :]
                r = tile.shape[0]
                pool.tensor_scalar(normed[0:r, 1, n, :], tile, moments[0:r, 1, n, 0:1],
                                   rstd[0:r, 1, n:n + 1], ALU.subtract, ALU.mult).then_inc(normed1_ready, 1)

            def run(pair, b, step, first, last):
                for n in range(TILES):
                    pool.wait_ge(recip_done, TILES * step + n + 1)
                    pool.tensor_tensor(probs[:, b, n, :], probs[:, b, n, :],
                                       recips[:, b, n:n + 1].to_broadcast([P, J]), ALU.mult) \
                        .then_inc(prob_done, 1)

            in_step(run)(pool)

            def split_w1(e):
                pool.tensor_copy(w1_hi[:, e, :], w1_sb[:, e, :]).then_inc(w1_hi_ready, 1)
                pool.wait_ge(w1_hi_ready, e + 1)
                pool.tensor_tensor(w1_lo[:, e, :], w1_sb[:, e, :], w1_hi[:, e, :].bitcast(F32), ALU.subtract) \
                    .then_inc(w1_split, 1)

            def scale_of(b):
                pool.wait_ge(var_ready, 2 * B + b + 1)
                pool.tensor_tensor(rstd[:, b, 0:QT], var_eps[:, b, 0:QT], half_power[:, 0:QT], ALU.pow) \
                    .then_inc(rstd_ready, 1)

            pool.wait_ge(w1_loaded, 16)
            for e in range(5):
                split_w1(e)
            scale_of(0)
            for e in range(5, E):
                split_w1(e)
            scale_of(1)


_INS = ['x', 'ctx_1024', 'L0_xattn_ln_m_g', 'L0_xattn_ln_m_b', 'L0_xattn_ln_l_g', 'L0_xattn_ln_l_b',
        'L0_xattn_Wq', 'L0_xattn_Wkv', 'L0_xattn_Wout', 'L0_ffn_Wg', 'L0_ffn_W1', 'L0_ffn_b1',
        'L0_ffn_W2', 'L0_ffn_b2']


def kernel(**inputs):
    import numpy as _np
    import concourse.bacc as _bacc
    from concourse import mybir as _mybir
    from concourse.bass_utils import run_bass_kernel_spmd as _run

    nc = _bacc.Bacc("TRN2", target_bir_lowering=False, num_devices=1)
    arrays, args = {}, []
    for name in _INS:
        a = _np.ascontiguousarray(inputs[name])
        arrays[f"in_{name}"] = a
        args.append(nc.dram_tensor(f"in_{name}", a.shape, _mybir.dt.from_np(a.dtype), kind="ExternalInput").ap())
    out = nc.dram_tensor("out_0", (B, N, D), _mybir.dt.float32, kind="ExternalOutput").ap()
    xattn_moe(nc, *args, out)
    r = _run(nc, [arrays], core_ids=[0])
    return r.results[0]["out_0"]
```

```python
from contextlib import ExitStack

import concourse.bass as bass
from concourse import mybir

F32 = mybir.dt.float32
F32R = mybir.dt.float32r
ALU = mybir.AluOpType
ACT = mybir.ActivationFunctionType
AX = mybir.AxisListType

P = 128
B, N, D = 2, 512, 128
M = 154
H, HD = 16, 64
PAIRS = H // 2
STEPS = PAIRS * B
J = N + M
JP = J + 2
JH = J // 2
QT = N // P
KT = 6
KP = J // KT
TILES = 2 * QT
CT = 2
CP = M // CT
E, HID, TOPK = 8, 256, 2
HC = HID // P
EPS = 1e-5
SCALE = HD ** -0.5

TURN_A = {n: 2 * n - 3 for n in range(2, TILES)}
PVS = {n: n - 4 for n in range(4, TILES)}
PVS_LATE = {0: KT - 2, 1: KT - 1}
UNITS = {0: "Q", 2: "K0", 4: "K1"}
V_UNITS = {5: "V0", 6: "V1", 7: "V2"}
TURN_B = {n: 2 * n - 2 for n in range(1, TILES - 1)}
O_COPY = 2
SPLIT_V = 5
SPLIT_QK = 5
W1_SPLITS = [(0, 0), (0, 2), (1, 0), (1, 2), (1, 4)]
SPREADS = 4
RING = 6


def unit_of(beat, odd, last):
    if last:
        return None
    return UNITS.get(beat) or (None if odd else V_UNITS.get(beat))


def values_before(pair, odd, b):
    return 3 * pair + 3 if odd else 3 * pair + 3 * b


def xattn_moe(nc, x, ctx_in, g_m, b_m, g_l, b_l, wq, wkv, wout, wg, w1, b1, w2, b2, out):
    with ExitStack() as stack:
        def sb(name, shape, dt=F32):
            return stack.enter_context(nc.sbuf_tensor(name, shape, dt))

        def ps(name, shape):
            return stack.enter_context(nc.psum_tensor(name, shape, F32))

        def sem(name):
            return stack.enter_context(nc.semaphore(name))

        x_tok = sb("x_tok", [P, B, QT, D])
        acc = x_tok
        ctx_tok = sb("ctx_tok", [CP, B, CT, D])
        rows = sb("rows", [E * HC + 4, P])
        cols = sb("cols", [P, E * HC + 4])
        ident = sb("ident", [P, P])
        earlier = sb("earlier", [P, E, E])
        half_power = sb("half_power", [P, QT + CT])
        stats = sb("stats", [P, B, QT + CT, 6])
        moments = sb("moments", [P, B, QT + CT, 2])
        var_eps = sb("var_eps", [P, B, QT + CT])
        rstd = sb("rstd", [P, B, QT + CT])
        normed = sb("normed", [P, B, QT + CT, D])
        kv_t = sb("kv_t", [P, B, JP])
        kv_hi = sb("kv_hi", [P, B, JP], F32R)
        kv_lo = sb("kv_lo", [P, B, JP], F32R)
        wqk_raw = sb("wqk_raw", [P, 2, P])
        wqk_hi = sb("wqk_hi", [P, 2, P], F32R)
        wqk_lo = sb("wqk_lo", [P, 2, P], F32R)
        wv_raw = sb("wv_raw", [P, 2 * P])
        wv_hi = sb("wv_hi", [P, 2 * P], F32R)
        wv_lo = sb("wv_lo", [P, 2 * P], F32R)
        q_st = sb("q_st", [P, B, 2, 2, N], F32R)
        q_pair = sb("q_pair", [P, B, 2, N], F32R)
        k_pair = sb("k_pair", [P, 2, JP], F32R)
        k_st = sb("k_st", [P, B, 2, JP], F32R)
        v_sb = sb("v_sb", [P, B, KT, 2 * P])
        neg_max = sb("neg_max", [P, B, TILES])
        sums = sb("sums", [P, B, TILES])
        recips = sb("recips", [P, B, TILES])
        probs = sb("probs", [P, B, TILES, J])
        ring = sb("ring", [P, RING, N])
        o_t = sb("o_t", [P, B, PAIRS, N])
        wout_sb = sb("wout_sb", [P, PAIRS, D])
        w1_raw = sb("w1_raw", [P, 2, HID])
        w1_hi = sb("w1_hi", [P, E, HID], F32R)
        w1_lo = sb("w1_lo", [P, E, HID], F32R)
        w2_sb = sb("w2_sb", [P, E * HC, D])
        wg_sb = sb("wg_sb", [P, E])
        b2_sb = sb("b2_sb", [E, D])
        g_neg = sb("g_neg", [P, B, QT])
        g_sub = sb("g_sub", [P, B, QT, E])
        g_exp = sb("g_exp", [P, B, QT, E])
        g_sum = sb("g_sum", [P, B, QT])
        g_rec = sb("g_rec", [P, B, QT])
        g_prob = sb("g_prob", [P, B, QT, E])
        g_gt = sb("g_gt", [P, QT, E, E])
        g_eq = sb("g_eq", [P, QT, E, E])
        g_rank = sb("g_rank", [P, B, QT, E])
        g_top = sb("g_top", [P, B, QT, E])
        g_tsum = sb("g_tsum", [P, B, QT])
        g_trec = sb("g_trec", [P, B, QT])
        score = sb("score", [P, B, QT, E])
        score_t = probs[0:E, 1, 0:B, 0:N]

        slots = ps("slots", [P, 2, 2, N])
        turned = ps("turned", [P, 2, N])
        proj = ps("proj", [P, N])
        o_ps = ps("o_ps", [P, N])
        first_k = [slots[:, 0, half, :] for half in range(2)]
        first_v = [o_ps[:, :], turned[:, 0, :], turned[:, 1, :]]
        logits_ps = [slots[:, 0, 1, :], o_ps]
        hid_ps = slots[:, :, :, :].rearrange("p a b n -> p (a b) n")

        x_in = [sem(f"x_in{b}") for b in range(B)]
        ctx_loaded = sem("ctx_loaded")
        rows_loaded = sem("rows_loaded")
        wqk_loaded = sem("wqk_loaded")
        wv_loaded = sem("wv_loaded")
        w1_loaded = [sem(f"w1_loaded{i}") for i in range(2)]
        tail_loaded = sem("tail_loaded")
        consts = sem("consts")
        cols_turned = sem("cols_turned")
        cols_ready = sem("cols_ready")
        setup_p = sem("setup_p")
        setup_v = sem("setup_v")
        var_ready = sem("var_ready")
        rstd_ready = sem("rstd_ready")
        normed_ready = sem("normed_ready")
        normed1_ready = sem("normed1_ready")
        norm_turned = sem("norm_turned")
        kv_ready = sem("kv_ready")
        kv_hi_ready = sem("kv_hi_ready")
        kv_lo_ready = sem("kv_lo_ready")
        wqk_hi_ready = sem("wqk_hi_ready")
        wqk_split = sem("wqk_split")
        wv_hi_ready = sem("wv_hi_ready")
        wv_split = sem("wv_split")
        scores_ready = sem("scores_ready")
        q_ready = sem("q_ready")
        k_ready = sem("k_ready")
        v_ready = sem("v_ready")
        max_done = sem("max_done")
        exp_done = sem("exp_done")
        recip_done = sem("recip_done")
        prob_done = sem("prob_done")
        q_hi_done = sem("q_hi_done")
        q_lo_done = sem("q_lo_done")
        spread_done = [[sem(f"spread_done{b}{h}") for h in range(2)] for b in range(B)]
        k_hi_done = sem("k_hi_done")
        k_lo_done = sem("k_lo_done")
        v_copied = sem("v_copied")
        turn_ready = sem("turn_ready")
        even_copied = sem("even_copied")
        odd_copied = sem("odd_copied")
        pv_done = sem("pv_done")
        o_copied = sem("o_copied")
        out_proj = sem("out_proj")
        x1_ready = sem("x1_ready")
        w1_split = sem("w1_split")
        w1_hi_ready = sem("w1_hi_ready")
        x2_turned = sem("x2_turned")
        x2_copied = sem("x2_copied")
        x2_hi = sem("x2_hi")
        x2_lo = sem("x2_lo")
        logits_ready = sem("logits_ready")
        gate_sub = sem("gate_sub")
        gate_exp = sem("gate_exp")
        score_ready = sem("score_ready")
        score_turned = sem("score_turned")
        score_copied = sem("score_copied")
        bias_ready = sem("bias_ready")
        acc_ready = sem("acc_ready")
        hid_ready = sem("hid_ready")
        relu_done = sem("relu_done")
        y_ready = sem("y_ready")
        acc_v = sem("acc_v")
        stored = sem("stored")

        block = stack.enter_context(nc.Block())

        wq_pair = wq.rearrange("d (r c) -> d r c", c=P)
        wkv_pair = wkv.rearrange("d (r c) -> d r c", c=P)
        wkv_two = wkv.rearrange("d (r c) -> d r c", c=2 * P)

        def in_step(run):
            def for_engine(eng):
                for b in range(B):
                    run(0, 0, b, b, b, False)
                with eng.Fori(1, PAIRS // 2) as two:
                    for odd in (1, 0):
                        pair = 2 * two - odd
                        for b in range(B):
                            run(pair, odd, b, 2 * pair + b, B, False)
                for b in range(B):
                    run(PAIRS - 1, 1, b, 2 * (PAIRS - 1) + b, B, b == B - 1)
            return for_engine

        @block.sync
        def _(sp):
            for b in range(B):
                sp.dma_start(x_tok[:, b], x[b].rearrange("(t p) d -> p t d", p=P)).then_inc(x_in[b], 16)
                if b == 0:
                    sp.dma_start(ctx_tok[:, :, :, :].rearrange("p b t d -> p (b t) d"),
                                 ctx_in.rearrange("b (t p) d -> p (b t) d", p=CP)).then_inc(ctx_loaded, 16)
            sp.dma_start(rows[0:E * HC, :], b1.rearrange("e (c p) -> (e c) p", p=P)).then_inc(rows_loaded, 16)
            sp.dma_start(wv_raw[:, :], wkv_two[:, PAIRS // 2]).then_inc(wv_loaded, 16)
            def load_qk(pair):
                sp.wait_ge(wqk_split, pair)
                sp.dma_start(wqk_raw[:, 0], wq_pair[:, bass.ds(pair, 1)]).then_inc(wqk_loaded, 16)
                sp.dma_start(wqk_raw[:, 1], wkv_pair[:, bass.ds(pair, 1)]).then_inc(wqk_loaded, 16)

            def load_v(two):
                sp.wait_ge(wv_split, 2 * two)
                sp.dma_start(wv_raw[:, :], wkv_two[:, bass.ds(two + PAIRS // 2, 1)]).then_inc(wv_loaded, 16)

            def double_q(b, h, step):
                sp.wait_ge(q_lo_done, step + 1)
                for half in range(2):
                    sp.dma_start(q_st[half * HD:(half + 1) * HD, b, h].bitcast(F32),
                                 q_pair[h * HD:(h + 1) * HD, b, :, :].bitcast(F32)) \
                      .then_inc(spread_done[b][h], 16)

            def stack_k(b, h, step):
                sp.wait_ge(k_lo_done, 2 * (step + 1))
                for part in range(2):
                    sp.dma_start(k_st[part * HD:(part + 1) * HD, b, h, :].bitcast(F32),
                                 k_pair[h * HD:(h + 1) * HD, part, :].bitcast(F32)) \
                      .then_inc(spread_done[b][h], 16)

            def spread(b, step):
                for h in range(2):
                    double_q(b, h, step)
                for h in range(2):
                    stack_k(b, h, step)

            def load_w1(e):
                if e >= 2:
                    sp.wait_ge(w1_split, e - 1)
                sp.dma_start(w1_raw[:, e % 2, :], w1[e]).then_inc(w1_loaded[e % 2], 16)

            for h in range(2):
                stack_k(0, h, 0)
                double_q(0, h, 0)
            load_qk(1)
            spread(1, 1)
            for e in range(2):
                load_w1(e)
            sp.dma_start(wout_sb[:, :, :], wout.rearrange("(r p) d -> p r d", p=P)).then_inc(tail_loaded, 16)
            sp.dma_start(w2_sb[:, :, :], w2.rearrange("e (c p) d -> p (e c) d", p=P)).then_inc(tail_loaded, 16)
            sp.dma_start(wg_sb[:, :], wg).then_inc(tail_loaded, 16)
            sp.dma_start(b2_sb[:, :], b2).then_inc(tail_loaded, 16)
            with sp.Fori(1, PAIRS // 2) as two:
                load_v(two)
                for odd in (1, 0):
                    pair = 2 * two - odd
                    spread(0, 2 * pair)
                    load_qk(pair + 1)
                    spread(1, 2 * pair + 1)
            spread(0, STEPS - 2)
            spread(1, STEPS - 1)
            for e in range(2, E):
                load_w1(e)
            for b in range(B):
                sp.wait_ge(acc_v, QT * E * (b + 1))
                sp.dma_start(out[b].rearrange("(t p) d -> p t d", p=P), acc[:, b]).then_inc(stored, 16)
            sp.wait_ge(stored, 16 * B)

        @block.tensor
        def _(pe):
            def three(out_ap, st_hi, st_lo, mv_hi, mv_lo):
                pe.matmul(out_ap, st_hi, mv_hi, start=True, stop=False)
                pe.matmul(out_ap, st_hi, mv_lo, start=False, stop=False)
                return pe.matmul(out_ap, st_lo, mv_hi, start=False, stop=True)

            def scores(pair, b, step, n, first):
                h, t, slot = n // QT, n % QT, n % 2
                if n < 2:
                    if first:
                        pe.wait_ge(exp_done, TILES * (step - 1) + n + 7)
                else:
                    pe.wait_ge(exp_done, TILES * step + n - 1)
                if t == 0 or (n == 2 and not first):
                    pe.wait_ge(spread_done[b][h], 16 * SPREADS * (pair + 1))
                for part in range(2):
                    for half in range(2):
                        mm = pe.matmul(slots[:, slot, half, 0:JH + 1], q_st[:, b, h, part, t * P:(t + 1) * P],
                                       k_st[:, b, h, half * JH:half * JH + JH + 1],
                                       start=(part == 0), stop=(part == 1))
                mm.then_inc(scores_ready, 1)

            def scores_unspread(n):
                if n == 0:
                    pe.wait_ge(k_lo_done, 2)
                    pe.wait_ge(q_lo_done, 1)
                else:
                    pe.wait_ge(kv_ready, 1 + 2 * B)
                for q_part in range(2):
                    for k_part in range(2):
                        for half in range(2):
                            mm = pe.matmul(slots[:, n, half, 0:JH + 1],
                                           q_pair[0:HD, 0, q_part, n * P:(n + 1) * P],
                                           k_pair[0:HD, k_part, half * JH:half * JH + JH + 1],
                                           start=(q_part + k_part == 0), stop=(q_part + k_part == 2))
                mm.then_inc(scores_ready, 1)

            def project_q(b):
                three(proj[:, :], wqk_hi[:, 0, :], wqk_lo[:, 0, :], kv_hi[:, b, 0:N], kv_lo[:, b, 0:N]) \
                    .then_inc(q_ready, 1)

            def project_k(b, half, bank=proj):
                at = slice(half * JP // 2, (half + 1) * JP // 2)
                three(bank[:, 0:JP // 2], wqk_hi[:, 1, :], wqk_lo[:, 1, :], kv_hi[:, b, at], kv_lo[:, b, at]) \
                    .then_inc(k_ready, 1)

            def project_v(b, third, bank):
                for k in range(2):
                    kt = third * 2 + k
                    at = slice(kt * KP, (kt + 1) * KP)
                    mm = three(bank[0:KP, k * 2 * P:(k + 1) * 2 * P], kv_hi[:, b, at], kv_lo[:, b, at],
                               wv_hi[:, :], wv_lo[:, :])
                mm.then_inc(v_ready, 1)

            def project(pair, odd, b, step, first, last, kind):
                values = values_before(pair, odd, b)
                if kind == "Q":
                    if first == 0 and b == 0:
                        pe.wait_ge(kv_lo_ready, 2 * B)
                    elif first == 1 or odd == b:
                        pe.wait_ge(k_lo_done, 2 * (step + 1))
                    else:
                        pe.wait_ge(v_copied, values)
                    pe.wait_ge(wqk_split, pair + b + 1)
                    project_q(1 - b)
                elif kind == "K0":
                    pe.wait_ge(q_lo_done, step + 2)
                    project_k(1 - b, 0)
                elif kind == "K1":
                    pe.wait_ge(k_lo_done, 2 * (step + 2) - 1)
                    project_k(1 - b, 1)
                elif first == 0:
                    if kind == "V0":
                        pe.wait_ge(wv_split, 2)
                    project_v(b, int(kind[1]), first_v[int(kind[1])])
                else:
                    if kind == "V0":
                        pe.wait_ge(k_lo_done, 2 * (step + 2))
                        pe.wait_ge(wv_split, pair + 2)
                    else:
                        pe.wait_ge(v_copied, values + int(kind[1]))
                    project_v(b, int(kind[1]), proj)

            def turn(b, of, i, no_earlier=False):
                kt, h = i // 2, i % 2
                if i < 2:
                    pe.wait_ge(prob_done, TILES * of + QT * (h + 1))
                g = i - 2
                if no_earlier and i < 2:
                    pe.wait_ge(v_copied, 3)
                if g >= 0 or not no_earlier:
                    pe.wait_ge(even_copied if g % 2 == 0 else odd_copied, 6 * of + g // 2 + 1)
                for t in range(QT):
                    mm = pe.transpose(turned[0:KP, i % 2, t * P:(t + 1) * P],
                                      probs[:, b, h * QT + t, kt * KP:(kt + 1) * KP], ident[:, :])
                mm.then_inc(turn_ready, 1)

            def pv(pair, odd, b, of, kt, no_earlier=False):
                if kt == 0:
                    if not odd:
                        pe.wait_ge(v_copied, values_before(pair, odd, b) + 3)
                    if not no_earlier:
                        pe.wait_ge(o_copied, of)
                pe.wait_ge(even_copied, 6 * of + kt + 1)
                pe.wait_ge(odd_copied, 6 * of + kt + 1)
                for h in range(2):
                    at = odd * P + h * HD
                    mm = pe.matmul(o_ps[h * HD:(h + 1) * HD, :], v_sb[0:KP, b, kt, at:at + HD],
                                   ring[0:KP, (2 * kt + h) % RING, :], start=(kt == 0), stop=(kt == KT - 1))
                mm.then_inc(pv_done, 1)

            pe.wait_ge(consts, 1)
            pe.wait_ge(rows_loaded, 16 * 5)
            pe.transpose(o_ps[:, 0:E * HC + 4], rows[:, :], ident[0:E * HC + 4, 0:E * HC + 4]) \
              .then_inc(cols_turned, 1)
            def turn_inputs(b, bank):
                normalised = normed1_ready if b else normed_ready
                for n in range(QT + CT):
                    pe.wait_ge(normalised, n + 1)
                    if n < QT:
                        mm = pe.transpose(bank[:, 0, n * P:(n + 1) * P], normed[:, b, n, :], ident[:, :])
                    else:
                        at = slice((n - QT) * CP, (n - QT + 1) * CP)
                        mm = pe.transpose(bank[:, 1, at], normed[0:CP, b, n, :], ident[0:CP, 0:CP])
                    if n in (QT - 1, QT + CT - 1):
                        mm.then_inc(norm_turned, 1)

            turn_inputs(0, turned)
            pe.wait_ge(kv_lo_ready, 1)
            pe.wait_ge(wqk_split, 1)
            project_k(0, 0, first_k[0])
            pe.wait_ge(kv_lo_ready, 2)
            project_k(0, 1, first_k[1])
            project_q(0)
            turn_inputs(1, slots[:, 1])

            def run(pair, odd, b, step, first, last):
                for n in range(TILES):
                    if first == 0 and b == 0 and n < 2:
                        if n == 0:
                            scores_unspread(0)
                            scores_unspread(1)
                    else:
                        scores(pair, b, step, n, first)
                    if n in PVS_LATE and first >= 2:
                        pv(pair - 1, 1 - odd, b, step - 2, PVS_LATE[n])
                    if first >= 1 and n in PVS:
                        of = (pair, odd) if b else (pair - 1, 1 - odd)
                        pv(*of, 1 - b, step - 1, PVS[n], no_earlier=(first == 1))
                    if first >= 1 and n in TURN_A:
                        turn(1 - b, step - 1, TURN_A[n], no_earlier=(first == 1))
                    if first >= 1 and n in TURN_B:
                        turn(1 - b, step - 1, TURN_B[n], no_earlier=(first == 1))
                    if unit_of(n, odd, last):
                        project(pair, odd, b, step, first, last, unit_of(n, odd, last))

            in_step(run)(pe)

            def out_project(b, bank, tiles):
                for t in tiles:
                    for r in range(PAIRS):
                        if t == 0 and r == PAIRS - 1:
                            pe.wait_ge(o_copied, STEPS - 1 + b)
                        mm = pe.matmul(bank[:, t * P:(t + 1) * P], o_t[:, b, r, t * P:(t + 1) * P],
                                       wout_sb[:, r, :], start=(r == 0), stop=(r == PAIRS - 1))
                if t == QT - 1:
                    mm.then_inc(out_proj, 1)

            def turn_x2(b):
                pe.wait_ge(normed_ready, QT + CT + QT * (b + 1))
                if b:
                    pe.wait_ge(acc_ready, 1)
                for t in range(QT):
                    mm = pe.transpose(proj[:, t * P:(t + 1) * P], normed[:, b, t, :], ident[:, :])
                mm.then_inc(x2_turned, 1)

            def logits(b):
                pe.wait_ge(x2_copied, b + 1)
                if b:
                    pe.wait_ge(score_copied, 1)
                for t in range(QT):
                    mm = pe.matmul(logits_ps[b][:, t * E:(t + 1) * E], kv_t[:, b, t * P:(t + 1) * P], wg_sb[:, :],
                                   start=True, stop=True)
                mm.then_inc(logits_ready, 1)

            def turn_scores(b):
                pe.wait_ge(score_ready, b + 1)
                for t in range(QT):
                    mm = pe.transpose(o_ps[0:E, t * P:(t + 1) * P], score[:, b, t, :], ident[:, :])
                mm.then_inc(score_turned, 1)

            def bias_term(b):
                pe.wait_ge(score_copied, b + 1)
                pe.wait_ge(x2_lo, b + 1)
                for t in range(QT):
                    mm = pe.matmul(proj[:, t * P:(t + 1) * P], score_t[:, b, t * P:(t + 1) * P],
                                   b2_sb[:, :], start=True, stop=True)
                mm.then_inc(bias_ready, 1)

            def hidden(g):
                b, e = g // E, g % E
                if e == 0:
                    pe.wait_ge(x2_lo, b + 1)
                pe.wait_ge(w1_split, min(g + 1, E))
                for c in range(HC):
                    n = g * HC + c
                    if n >= 4:
                        pe.wait_ge(relu_done, n - 3)
                    elif n == 0:
                        pe.wait_ge(x1_ready, 1)
                    elif n == 1:
                        pe.wait_ge(gate_sub, 1)
                    elif n == 2:
                        pe.wait_ge(x1_ready, 2)
                    three(hid_ps[:, n % 4, :], w1_hi[:, e, c * P:(c + 1) * P], w1_lo[:, e, c * P:(c + 1) * P],
                          kv_hi[:, b, 0:N], kv_lo[:, b, 0:N]).then_inc(hid_ready, 1)

            def expert_out(g):
                e = g % E
                if g >= 2:
                    pe.wait_ge(acc_v, QT * (g - 1))
                elif g == 0:
                    pe.wait_ge(odd_copied, 6 * STEPS)
                pe.wait_ge(relu_done, HC * (g + 1))
                for t in range(QT):
                    for c in range(HC):
                        mm = pe.matmul(turned[:, g % 2, t * P:(t + 1) * P],
                                       ring[:, (g * HC + c) % RING, t * P:(t + 1) * P],
                                       w2_sb[:, e * HC + c, :], start=(c == 0), stop=(c == HC - 1))
                mm.then_inc(y_ready, 1)

            pv(PAIRS - 1, 1, 0, STEPS - 2, KT - 2)
            pv(PAIRS - 1, 1, 0, STEPS - 2, KT - 1)
            turn(1, STEPS - 1, 0)
            pe.wait_ge(tail_loaded, 16 * 4)
            pe.wait_ge(exp_done, TILES * STEPS - 1)
            out_project(0, slots[:, 0, 0, :], range(0, QT // 2))
            turn(1, STEPS - 1, 1)
            out_project(0, slots[:, 0, 0, :], range(QT // 2, QT))
            for i in range(2, 2 * KT):
                turn(1, STEPS - 1, i)
                if i >= 3 and i % 2 == 1:
                    pv(PAIRS - 1, 1, 1, STEPS - 1, i // 2 - 1)
            turn_x2(0)
            pv(PAIRS - 1, 1, 1, STEPS - 1, KT - 1)
            pe.wait_ge(exp_done, TILES * STEPS)
            logits(0)
            out_project(1, slots[:, 1, 0, :], range(QT))
            for g in range(B * E):
                hidden(g)
                if g % E == 1:
                    turn_scores(g // E)
                if g >= 1:
                    expert_out(g - 1)
                if g % E == 1:
                    bias_term(g // E)
                if g == E // 2:
                    turn_x2(1)
                if g == E // 2 + 1:
                    logits(1)
            expert_out(B * E - 1)

        @block.scalar
        def _(act):
            act.dma_start(wqk_raw[:, 1], wkv_pair[:, 0]).then_inc(wqk_loaded, 16)
            act.dma_start(wqk_raw[:, 0], wq_pair[:, 0]).then_inc(wqk_loaded, 16)
            for n, v in enumerate([g_l, b_l, g_m, b_m]):
                act.dma_start(rows[E * HC + n:E * HC + n + 1, :], v.rearrange("(a d) -> a d", a=1)) \
                   .then_inc(rows_loaded, 16)
            def split_qk(n):
                act.wait_ge(wqk_loaded, 32 * (n + 1))
                act.copy(wqk_hi[:, :, :], wqk_raw[:, :, :]).then_inc(wqk_hi_ready, 1)

            def split_v(pair):
                act.wait_ge(wv_loaded, 8 * (pair + 2))
                act.copy(wv_hi[:, :], wv_raw[:, :]).then_inc(wv_hi_ready, 2)

            def q_high(b, step):
                act.wait_ge(q_ready, step + 1)
                act.activation(q_pair[:, b, 0, :], proj[:, :], ACT.Copy, scale=SCALE).then_inc(q_hi_done, 1)

            def k_high(step, half, before=None, bank=proj):
                act.wait_ge(k_ready, 2 * step + half + 1)
                if half == 0 and before:
                    pair, b = before
                    for h in range(2):
                        act.wait_ge(spread_done[b][h], 16 * SPREADS * (pair + 1))
                at = slice(half * JP // 2, (half + 1) * JP // 2)
                act.copy(k_pair[:, 0, at], bank[:, 0:JP // 2]).then_inc(k_hi_done, 1)

            def copy_v(pair, odd, b, third, bank):
                act.wait_ge(v_ready, values_before(pair, odd, b) + third + 1)
                kts = slice(third * 2, third * 2 + 2)
                act.copy(v_sb[0:KP, b, kts].rearrange("p k c -> p (k c)"), bank[0:KP, :]).then_inc(v_copied, 1)

            def copy_turned(of, i, no_earlier):
                act.wait_ge(turn_ready, 2 * KT * of + i + 1)
                if not (no_earlier and i < RING):
                    act.wait_ge(pv_done, KT * of + (i - RING) // 2 + 1)
                act.copy(ring[0:KP, i % RING, :], turned[0:KP, i % 2, :]).then_inc(even_copied, 1)

            act.wait_ge(cols_turned, 1)
            act.copy(cols[:, :], o_ps[:, 0:E * HC + 4]).then_inc(cols_ready, 1)
            split_qk(0)
            split_v(0)
            def inputs_high(b):
                for i, at in enumerate([slice(0, N), slice(N, JP)]):
                    act.wait_ge(kv_ready, 2 * b + i + 2)
                    act.copy(kv_hi[:, b, at], kv_t[:, b, at]).then_inc(kv_hi_ready, 1)

            inputs_high(0)
            k_high(0, 0, bank=first_k[0])
            k_high(0, 1, bank=first_k[1])
            q_high(0, 0)
            inputs_high(1)

            def copy_output(b, of, pair):
                act.wait_ge(pv_done, KT * (of + 1))
                if isinstance(pair, int):
                    to = o_t[:, b, pair, :]
                else:
                    to = o_t[:, b, bass.ds(pair, 1), :].rearrange("p a n -> p (a n)")
                act.copy(to, o_ps[:, :]).then_inc(o_copied, 1)

            def run(pair, odd, b, step, first, last):
                for n in range(TILES):
                    kind = unit_of(n, odd, last)
                    act.wait_ge(max_done, TILES * step + n + 1)
                    act.activation(probs[:, b, n, :].rearrange("p (a n) -> p a n", a=2),
                                   slots[:, n % 2, :, 0:JH], ACT.Exp, bias=neg_max[:, b, n:n + 1],
                                   accum_out=sums[:, b, n:n + 1]).then_inc(exp_done, 1)
                    if first >= 1 and n in TURN_B:
                        copy_turned(step - 1, TURN_B[n], first == 1)
                    if kind == "Q":
                        q_high(1 - b, step + 1)
                    elif kind and kind[0] == "K":
                        k_high(step + 1, int(kind[1]), before=(pair, b))
                    elif kind:
                        third = int(kind[1])
                        copy_v(pair, odd, b, third, first_v[third] if first == 0 else proj)
                    if n == O_COPY and first >= 2:
                        copy_output(b, step - 2, pair - 1)
                    if b == 0 and n == SPLIT_V and odd and not isinstance(pair, int):
                        act.wait_ge(v_ready, values_before(pair, odd, b))
                        split_v(pair + 1)
                    if b == 0 and n == SPLIT_QK and not (first == B and isinstance(pair, int)):
                        act.wait_ge(k_ready, 2 * (step + 2))
                        split_qk(pair + 1)

            in_step(run)(act)
            copy_output(0, STEPS - 2, PAIRS - 1)
            for i in range(0, 2 * KT, 2):
                copy_turned(STEPS - 1, i, False)

            def gate_exp_of(b):
                act.wait_ge(gate_sub, b + 1)
                act.activation(g_exp[:, b], g_sub[:, b], ACT.Exp).then_inc(gate_exp, 1)

            def copy_x2(b):
                act.wait_ge(x2_turned, b + 1)
                act.copy(kv_t[:, b, 0:N], proj[:, :]).then_inc(x2_copied, 1)
                act.copy(kv_hi[:, b, 0:N], proj[:, :]).then_inc(x2_hi, 1)

            def relu(n):
                act.wait_ge(hid_ready, n + 1)
                if n >= RING:
                    act.wait_ge(y_ready, (n - RING) // HC + 1)
                act.activation(ring[:, n % RING, :], hid_ps[:, n % 4, :], ACT.Relu,
                               bias=cols[:, n % (E * HC):n % (E * HC) + 1]).then_inc(relu_done, 1)

            def copy_scores(b):
                act.wait_ge(score_turned, b + 1)
                act.copy(score_t[:, b, :], o_ps[0:E, :]).then_inc(score_copied, 1)

            copy_x2(0)
            copy_output(1, STEPS - 1, PAIRS - 1)
            gate_exp_of(0)
            act.wait_ge(pv_done, KT * STEPS)
            for g in range(B * E):
                for c in range(HC):
                    relu(g * HC + c)
                if g % E == 1:
                    copy_scores(g // E)
                if g == E // 2:
                    copy_x2(1)
                if g == E // 2 + 1:
                    gate_exp_of(1)

        @block.vector
        def _(dve):
            own = [0]

            def chained(op):
                op.then_inc(setup_v, 1)
                own[0] += 1
                dve.wait_ge(setup_v, own[0])

            def moments_of(b, tiles):
                for n, tile in tiles:
                    ins = dve.bn_stats(stats[0:tile.shape[0], b, n, :], tile)
                chained(ins)
                for n, tile in tiles:
                    ins = dve.bn_aggr(moments[0:tile.shape[0], b, n, :], stats[0:tile.shape[0], b, n, :])
                chained(ins)

            def apply_norm(b, tiles):
                for n, tile in tiles:
                    r = tile.shape[0]
                    dve.tensor_scalar(normed[0:r, b, n, :], tile, moments[0:r, b, n, 0:1],
                                      rstd[0:r, b, n:n + 1], ALU.subtract, ALU.mult).then_inc(normed_ready, 1)

            def q_low(b, step):
                dve.wait_ge(q_hi_done, step + 1)
                dve.scalar_tensor_tensor(q_pair[:, b, 1, :], proj[:, :], SCALE, q_pair[:, b, 0, :].bitcast(F32),
                                         ALU.mult, ALU.subtract).then_inc(q_lo_done, 1)

            def k_low(step, half, bank=proj):
                dve.wait_ge(k_hi_done, 2 * step + half + 1)
                at = slice(half * JP // 2, (half + 1) * JP // 2)
                dve.tensor_tensor(k_pair[:, 1, at], bank[:, 0:JP // 2], k_pair[:, 0, at].bitcast(F32),
                                  ALU.subtract).then_inc(k_lo_done, 1)

            chained(dve.memset(moments[:, :, :, :], 1.0))
            dve.memset(kv_t[:, :, J:JP], 0.0).then_inc(kv_ready, 1)
            def input_tiles(b):
                return [(t, x_tok[:, b, t, :]) for t in range(QT)] + \
                       [(QT + t, ctx_tok[:, b, t, :]) for t in range(CT)]

            for b in range(B):
                dve.wait_ge(x_in[b], 16)
                dve.wait_ge(ctx_loaded, 16)
                moments_of(b, input_tiles(b))
                dve.tensor_scalar(var_eps[:, b, 0:QT], moments[:, b, 0:QT, 1], 1.0 + EPS, EPS * EPS,
                                  ALU.mult, ALU.add).then_inc(var_ready, 1)
                dve.tensor_scalar(var_eps[:, b, QT:QT + CT], moments[:, b, QT:QT + CT, 1], EPS, None,
                                  ALU.add).then_inc(var_ready, 1)
            dve.wait_ge(rstd_ready, 1)
            apply_norm(0, input_tiles(0))
            def inputs_gained(b, bank):
                dve.wait_ge(norm_turned, 2 * b + 1)
                g = E * HC
                dve.tensor_scalar(kv_t[:, b, 0:N], bank[:, 0, :], cols[:, g:g + 1], cols[:, g + 1:g + 2],
                                  ALU.mult, ALU.add).then_inc(kv_ready, 1)
                dve.wait_ge(norm_turned, 2 * b + 2)
                dve.tensor_scalar(kv_t[:, b, N:J], bank[:, 1, 0:M], cols[:, g + 2:g + 3],
                                  cols[:, g + 3:g + 4], ALU.mult, ALU.add).then_inc(kv_ready, 1)

            def inputs_low(b):
                for i, at in enumerate([slice(0, N), slice(N, JP)]):
                    dve.wait_ge(kv_hi_ready, 2 * b + i + 1)
                    dve.tensor_tensor(kv_lo[:, b, at], kv_t[:, b, at], kv_hi[:, b, at].bitcast(F32),
                                      ALU.subtract).then_inc(kv_lo_ready, 1)

            dve.wait_ge(cols_ready, 1)
            inputs_gained(0, turned)
            dve.wait_ge(wqk_hi_ready, 1)
            dve.tensor_tensor(wqk_lo[:, :, :], wqk_raw[:, :, :], wqk_hi[:, :, :].bitcast(F32),
                              ALU.subtract).then_inc(wqk_split, 1)
            dve.wait_ge(wv_hi_ready, 1)
            dve.tensor_tensor(wv_lo[:, :], wv_raw[:, :], wv_hi[:, :].bitcast(F32),
                              ALU.subtract).then_inc(wv_split, 2)
            inputs_low(0)
            k_low(0, 0, bank=first_k[0])
            k_low(0, 1, bank=first_k[1])
            q_low(0, 0)
            inputs_gained(1, slots[:, 1])

            def copy_turned(of, i, no_earlier):
                dve.wait_ge(turn_ready, 2 * KT * of + i + 1)
                if not (no_earlier and i < RING):
                    dve.wait_ge(pv_done, KT * of + (i - RING) // 2 + 1)
                dve.tensor_copy(ring[0:KP, i % RING, :], turned[0:KP, i % 2, :]).then_inc(odd_copied, 1)

            def reciprocal(b, step, n):
                dve.wait_ge(exp_done, TILES * step + n + 1)
                dve.reciprocal(recips[:, b, n:n + 1], sums[:, b, n:n + 1]).then_inc(recip_done, 1)

            def run(pair, odd, b, step, first, last):
                for n in range(TILES):
                    dve.wait_ge(scores_ready, TILES * step + n + 1)
                    dve.tensor_reduce(neg_max[:, b, n:n + 1], slots[:, n % 2, :, 0:JH], AX.XY, ALU.max,
                                      negate=True).then_inc(max_done, 1)
                    if first == 0 and b == 0 and n == 0:
                        inputs_low(1)
                    before = unit_of(n - 1, odd, last)
                    if before == "Q":
                        q_low(1 - b, step + 1)
                    elif before and before[0] == "K":
                        k_low(step + 1, int(before[1]))
                    if first >= 1 and n in TURN_A:
                        copy_turned(step - 1, TURN_A[n], first == 1)
                    if n >= 1:
                        reciprocal(b, step, n - 1)
                    elif first >= 1:
                        reciprocal(1 - b, step - 1, TILES - 1)
                    if b == 0 and n == SPLIT_V + 1 and odd and not isinstance(pair, int):
                        dve.wait_ge(wv_hi_ready, pair + 3)
                        dve.tensor_tensor(wv_lo[:, :], wv_raw[:, :], wv_hi[:, :].bitcast(F32),
                                          ALU.subtract).then_inc(wv_split, 2)
                    if b == 0 and n == SPLIT_QK + 1 and not (first == B and isinstance(pair, int)):
                        dve.wait_ge(wqk_hi_ready, pair + 2)
                        dve.tensor_tensor(wqk_lo[:, :, :], wqk_raw[:, :, :], wqk_hi[:, :, :].bitcast(F32),
                                          ALU.subtract).then_inc(wqk_split, 1)

            in_step(run)(dve)
            reciprocal(1, STEPS - 1, TILES - 1)

            def x1_and_moments(b, bank):
                dve.wait_ge(out_proj, b + 1)
                dve.tensor_tensor(acc[:, b].rearrange("p t d -> p (t d)"), bank,
                                  x_tok[:, b].rearrange("p t d -> p (t d)"), ALU.add).then_inc(x1_ready, 1)
                dve.wait_ge(x1_ready, b + 1)
                moments_of(b, [(t, acc[:, b, t, :]) for t in range(QT)])
                dve.tensor_scalar(var_eps[:, b, 0:QT], moments[:, b, 0:QT, 1], EPS, None, ALU.add) \
                   .then_inc(var_ready, 1)

            def norm_x1(b):
                dve.wait_ge(rstd_ready, B + b + 1)
                apply_norm(b, [(t, acc[:, b, t, :]) for t in range(QT)])

            def split_x2(b):
                dve.wait_ge(x2_hi, b + 1)
                dve.tensor_tensor(kv_lo[:, b, 0:N], proj[:, :], kv_hi[:, b, 0:N].bitcast(F32),
                                  ALU.subtract).then_inc(x2_lo, 1)

            def gate_start(b):
                dve.wait_ge(logits_ready, b + 1)
                lg = logits_ps[b][:, 0:QT * E].rearrange("p (t e) -> p t e", e=E)
                chained(dve.tensor_reduce(g_neg[:, b, :], lg, AX.X, ALU.max))
                dve.tensor_tensor(g_sub[:, b], lg, g_neg[:, b, :].unsqueeze(2).to_broadcast([P, QT, E]),
                                  ALU.subtract).then_inc(gate_sub, 1)

            def gate_end(b):
                dve.wait_ge(gate_exp, b + 1)
                chained(dve.tensor_reduce(g_sum[:, b, :], g_exp[:, b], AX.X, ALU.add))
                chained(dve.reciprocal(g_rec[:, b, :], g_sum[:, b, :]))
                chained(dve.tensor_tensor(g_prob[:, b], g_exp[:, b],
                                          g_rec[:, b, :].unsqueeze(2).to_broadcast([P, QT, E]), ALU.mult))
                for t in range(QT):
                    pj = g_prob[:, b, t, :].unsqueeze(1).to_broadcast([P, E, E])
                    pe_ = g_prob[:, b, t, :].unsqueeze(2).to_broadcast([P, E, E])
                    dve.tensor_tensor(g_gt[:, t], pj, pe_, ALU.is_gt)
                    ins = dve.tensor_tensor(g_eq[:, t], pj, pe_, ALU.is_equal)
                chained(ins)
                first_of = earlier[:, :, :].unsqueeze(1).to_broadcast([P, QT, E, E])
                chained(dve.tensor_tensor(g_eq[:, :], g_eq[:, :], first_of, ALU.mult))
                chained(dve.tensor_tensor(g_gt[:, :], g_gt[:, :], g_eq[:, :], ALU.add))
                chained(dve.tensor_reduce(g_rank[:, b], g_gt[:, :], AX.X, ALU.add))
                chained(dve.scalar_tensor_tensor(g_top[:, b], g_rank[:, b], float(TOPK), g_prob[:, b],
                                                 ALU.is_lt, ALU.mult))
                chained(dve.tensor_reduce(g_tsum[:, b, :], g_top[:, b], AX.X, ALU.add))
                chained(dve.reciprocal(g_trec[:, b, :], g_tsum[:, b, :]))
                dve.tensor_tensor(score[:, b], g_top[:, b],
                                  g_trec[:, b, :].unsqueeze(2).to_broadcast([P, QT, E]), ALU.mult) \
                   .then_inc(score_ready, 1)

            def add_bias(b):
                dve.wait_ge(bias_ready, b + 1)
                dve.tensor_tensor(acc[:, b].rearrange("p t d -> p (t d)"), proj[:, :],
                                  acc[:, b].rearrange("p t d -> p (t d)"), ALU.add).then_inc(acc_ready, 1)
                dve.wait_ge(acc_ready, b + 1)

            def add_expert(g):
                b, e = g // E, g % E
                dve.wait_ge(y_ready, g + 1)
                if e >= 1:
                    dve.wait_ge(acc_v, QT * g)
                for t in range(QT):
                    dve.scalar_tensor_tensor(acc[:, b, t, :], turned[:, g % 2, t * P:(t + 1) * P],
                                             score[:, b, t, e:e + 1], acc[:, b, t, :], ALU.mult, ALU.add) \
                       .then_inc(acc_v, 1)

            copy_turned(STEPS - 1, 1, False)
            x1_and_moments(0, slots[:, 0, 0, :])
            copy_turned(STEPS - 1, 3, False)
            copy_turned(STEPS - 1, 5, False)
            norm_x1(0)
            for i in range(7, 2 * KT, 2):
                copy_turned(STEPS - 1, i, False)
            gate_start(0)
            split_x2(0)
            gate_end(0)
            x1_and_moments(1, slots[:, 1, 0, :])
            norm_x1(1)
            for g in range(B * E):
                if g % E == 0:
                    add_bias(g // E)
                add_expert(g)
                if g == E // 2 - 1:
                    split_x2(1)
                if g == E // 2:
                    gate_start(1)
                    gate_end(1)

        @block.gpsimd
        def _(pool):
            pool.memset(ident[:, :], 0.0).then_inc(setup_p, 1)
            pool.memset(earlier[:, :, :], 1.0).then_inc(setup_p, 1)
            pool.memset(half_power[:, :], -0.5).then_inc(setup_p, 1)
            pool.wait_ge(setup_p, 3)
            pool.affine_select(out=ident[:, :], in_=ident[:, :], compare_op=ALU.not_equal, fill=1.0,
                               base=0, pattern=[[-1, P]], channel_multiplier=1).then_inc(consts, 1)
            pool.affine_select(out=earlier[:, :, :], in_=earlier[:, :, :], compare_op=ALU.is_ge, fill=0.0,
                               base=-1, pattern=[[1, E], [-1, E]], channel_multiplier=0).then_inc(consts, 1)

            for b in range(B):
                pool.wait_ge(var_ready, 2 * (b + 1))
                pool.tensor_tensor(rstd[:, b, :], var_eps[:, b, :], half_power[:, :], ALU.pow) \
                    .then_inc(rstd_ready, 1)
            pool.wait_ge(rstd_ready, B)
            for n in range(QT + CT):
                tile = x_tok[:, 1, n, :] if n < QT else ctx_tok[:, 1, n - QT, :]
                r = tile.shape[0]
                pool.tensor_scalar(normed[0:r, 1, n, :], tile, moments[0:r, 1, n, 0:1],
                                   rstd[0:r, 1, n:n + 1], ALU.subtract, ALU.mult).then_inc(normed1_ready, 1)

            def split_w1(e):
                pool.wait_ge(w1_loaded[e % 2], 16 * (e // 2 + 1))
                pool.tensor_copy(w1_hi[:, e, :], w1_raw[:, e % 2, :]).then_inc(w1_hi_ready, 1)
                pool.wait_ge(w1_hi_ready, e + 1)
                pool.tensor_tensor(w1_lo[:, e, :], w1_raw[:, e % 2, :], w1_hi[:, e, :].bitcast(F32), ALU.subtract) \
                    .then_inc(w1_split, 1)

            def run(pair, odd, b, step, first, last):
                for n in range(TILES):
                    pool.wait_ge(recip_done, TILES * step + n + 1)
                    pool.tensor_tensor(probs[:, b, n, :], probs[:, b, n, :],
                                       recips[:, b, n:n + 1].to_broadcast([P, J]), ALU.mult) \
                        .then_inc(prob_done, 1)
                    if isinstance(pair, int) and pair == PAIRS - 1 and (b, n) in W1_SPLITS:
                        split_w1(W1_SPLITS.index((b, n)))

            in_step(run)(pool)
            for e in range(len(W1_SPLITS), E):
                split_w1(e)
            for b in range(B):
                pool.wait_ge(var_ready, 2 * B + b + 1)
                pool.tensor_tensor(rstd[:, b, 0:QT], var_eps[:, b, 0:QT], half_power[:, 0:QT], ALU.pow) \
                    .then_inc(rstd_ready, 1)


_INS = ['x', 'ctx_1024', 'L0_xattn_ln_m_g', 'L0_xattn_ln_m_b', 'L0_xattn_ln_l_g', 'L0_xattn_ln_l_b',
        'L0_xattn_Wq', 'L0_xattn_Wkv', 'L0_xattn_Wout', 'L0_ffn_Wg', 'L0_ffn_W1', 'L0_ffn_b1',
        'L0_ffn_W2', 'L0_ffn_b2']


def kernel(**inputs):
    import numpy as _np
    import concourse.bacc as _bacc
    from concourse import mybir as _mybir
    from concourse.bass_utils import run_bass_kernel_spmd as _run

    nc = _bacc.Bacc("TRN2", target_bir_lowering=False, num_devices=1)
    arrays, args = {}, []
    for name in _INS:
        a = _np.ascontiguousarray(inputs[name])
        arrays[f"in_{name}"] = a
        args.append(nc.dram_tensor(f"in_{name}", a.shape, _mybir.dt.from_np(a.dtype), kind="ExternalInput").ap())
    out = nc.dram_tensor("out_0", (B, N, D), _mybir.dt.float32, kind="ExternalOutput").ap()
    xattn_moe(nc, *args, out)
    r = _run(nc, [arrays], core_ids=[0])
    return r.results[0]["out_0"]
```
